# Optimizing a Trainium2 kernel written in Bass

```python
import numpy as np
import jax
import jax.numpy as jnp

def _softmax(x, axis=-1):
    return jax.nn.softmax(x, axis=axis)

def _gelu(x):
    return jax.nn.gelu(x, approximate=True)

def _silu(x):
    return jax.nn.silu(x)

def _sigmoid(x):
    return jax.nn.sigmoid(x)

def _layernorm(x, axis=-1, eps=1e-05):
    m = jnp.mean(x, axis=axis, keepdims=True)
    v = jnp.var(x, axis=axis, keepdims=True)
    return (x - m) / jnp.sqrt(v + eps)

def _scatter_add(tgt, idx, src, axis=0):
    return tgt.at[idx].add(src)

def _segment_sum(src, seg, n):
    return jax.ops.segment_sum(src, seg, n)
kernel_name = 'mk_cond_resid_d2_seqx_r8_e240fc'

def setup_inputs(seed: int=0):
    np.random.seed(seed)
    _w = jnp.asarray

    def _rec_inputs():
        import jax
        import jax.numpy as jnp
        _rk = jax.random.key(seed)
        x = -7.109e-05 + 0.9999 * jax.random.normal(jax.random.fold_in(_rk, 1), (32, 32, 256), jnp.float32)
        _lenS = 32 - jax.random.randint(jax.random.fold_in(_rk, 7), (32,), 0, max(1, 32 // 4) + 1, jnp.int32)
        _lenS2 = 32 - jax.random.randint(jax.random.fold_in(_rk, 8), (32,), 0, max(1, 32 // 4) + 1, jnp.int32)
        itok_B_1_198 = jax.random.randint(jax.random.fold_in(_rk, 11), (32,), 1, 199, jnp.int32)
        itok_Bx257_0_4111 = jax.random.randint(jax.random.fold_in(_rk, 12), (32, 257), 0, 514, jnp.int32)
        itok_B_37_3939 = jax.random.randint(jax.random.fold_in(_rk, 13), (32,), 37, 3940, jnp.int32)
        return (x, itok_B_1_198, itok_Bx257_0_4111, itok_B_37_3939)
    x, itok_B_1_198, itok_Bx257_0_4111, itok_B_37_3939 = _rec_inputs()

    def _L0_cond_setup():
        import jax, jax.numpy as jnp
        import numpy as np
        B, C, T = (128, 32, 256)
        S, D = (200, 32)
        key = jax.random.key(seed)
        k1, k2, k3 = jax.random.split(key, 3)
        x = jax.random.normal(k1, (B, C, T), dtype=jnp.float32)
        conditions = jax.random.randint(k2, (B,), 0, S, dtype=jnp.int64)
        weights = jax.random.normal(k3, (S, C, D), dtype=jnp.float32) / jnp.sqrt(jnp.float32(C))
        return {'x': x, 'conditions': conditions, 'weights': weights}
    _L0_cond_all = _L0_cond_setup()
    _L0_cond_in = {k: v for k, v in _L0_cond_all.items() if k in ('weights',)}
    del _L0_cond_all

    def _L1_cond_setup():
        import jax, jax.numpy as jnp
        import numpy as np
        H, G, HD = (8, 4, 32)
        GSZ = H // G
        BLOCK = 16
        WINDOW = 128
        SCALE = 256.0 ** (-0.5)
        EPS = 1e-06
        THETA = 10000.0
        B, T, D = (16, 4, 256)
        NBLK = 257

        def _rms(x, scale):
            var = jnp.mean(x * x, axis=-1, keepdims=True)
            return x * jax.lax.rsqrt(var + EPS) * (1.0 + scale)

        def _rope(x, pos):
            half = HD // 2
            inv = 1.0 / THETA ** (jnp.arange(half, dtype=jnp.float32) / half)
            ang = pos[:, :, None].astype(jnp.float32) * inv
            cos = jnp.cos(ang)[:, None, :, :]
            sin = jnp.sin(ang)[:, None, :, :]
            x1, x2 = (x[..., :half], x[..., half:])
            return jnp.concatenate([x1 * cos - x2 * sin, x2 * cos + x1 * sin], axis=-1)
        key = jax.random.key(seed)
        ks = jax.random.split(key, 10)
        inv_d = 1.0 / np.sqrt(D)
        return {'x': jax.random.normal(ks[0], (B, T, D), jnp.float32), 'Wq': jax.random.normal(ks[1], (H * HD, D), jnp.float32) * inv_d, 'Wk': jax.random.normal(ks[2], (G * HD, D), jnp.float32) * inv_d, 'Wv': jax.random.normal(ks[3], (G * HD, D), jnp.float32) * inv_d, 'Wo': jax.random.normal(ks[4], (D, H * HD), jnp.float32) * inv_d, 'q_norm_scale': jax.random.normal(ks[5], (HD,), jnp.float32) * 0.02, 'k_norm_scale': jax.random.normal(ks[6], (HD,), jnp.float32) * 0.02, 'k_blocks': jax.random.normal(ks[7], (B * NBLK, G, BLOCK, HD), jnp.float32), 'v_blocks': jax.random.normal(ks[8], (B * NBLK, G, BLOCK, HD), jnp.float32), 'block_tables': jnp.arange(B * NBLK, dtype=jnp.int32).reshape(B, NBLK), 'kv_lens': jax.random.randint(ks[9], (B,), 0, 512, dtype=jnp.int32)}
    _L1_cond_all = _L1_cond_setup()
    _L1_cond_in = {k: v for k, v in _L1_cond_all.items() if k in ('Wq', 'Wk', 'Wv', 'Wo', 'q_norm_scale', 'k_norm_scale', 'k_blocks', 'v_blocks')}
    del _L1_cond_all
    return {'x': x, 'itok_B_1_198': itok_B_1_198, 'itok_Bx257_0_4111': itok_Bx257_0_4111, 'itok_B_37_3939': itok_B_37_3939, 'L0_cond_weights': _L0_cond_in['weights'], 'L1_cond_Wq': _L1_cond_in['Wq'], 'L1_cond_Wk': _L1_cond_in['Wk'], 'L1_cond_Wv': _L1_cond_in['Wv'], 'L1_cond_Wo': _L1_cond_in['Wo'], 'L1_cond_q_norm_scale': _L1_cond_in['q_norm_scale'], 'L1_cond_k_norm_scale': _L1_cond_in['k_norm_scale'], 'L1_cond_k_blocks': _L1_cond_in['k_blocks'], 'L1_cond_v_blocks': _L1_cond_in['v_blocks']}

def reference(x, itok_B_1_198, itok_Bx257_0_4111, itok_B_37_3939, L0_cond_weights, L1_cond_Wq, L1_cond_Wk, L1_cond_Wv, L1_cond_Wo, L1_cond_q_norm_scale, L1_cond_k_norm_scale, L1_cond_k_blocks, L1_cond_v_blocks):
    import jax
    import jax.numpy as jnp

    def _L0_cond_ref(x, conditions, weights):
        import jax, jax.numpy as jnp
        import numpy as np
        B, C, T = (128, 32, 256)
        S, D = (200, 32)
        w = weights[conditions]
        return jnp.einsum('bct,bcd->bdt', x, w)

    def _L1_cond_ref(x, Wq, Wk, Wv, Wo, q_norm_scale, k_norm_scale, k_blocks, v_blocks, block_tables, kv_lens):
        import jax, jax.numpy as jnp
        import numpy as np
        H, G, HD = (8, 4, 32)
        GSZ = H // G
        BLOCK = 16
        WINDOW = 128
        SCALE = 256.0 ** (-0.5)
        EPS = 1e-06
        THETA = 10000.0
        B, T, D = (16, 4, 256)
        NBLK = 257

        def _rms(x, scale):
            var = jnp.mean(x * x, axis=-1, keepdims=True)
            return x * jax.lax.rsqrt(var + EPS) * (1.0 + scale)

        def _rope(x, pos):
            half = HD // 2
            inv = 1.0 / THETA ** (jnp.arange(half, dtype=jnp.float32) / half)
            ang = pos[:, :, None].astype(jnp.float32) * inv
            cos = jnp.cos(ang)[:, None, :, :]
            sin = jnp.sin(ang)[:, None, :, :]
            x1, x2 = (x[..., :half], x[..., half:])
            return jnp.concatenate([x1 * cos - x2 * sin, x2 * cos + x1 * sin], axis=-1)
        Bx, Tx, _ = x.shape
        q = jnp.einsum('btd,od->bto', x, Wq).reshape(Bx, Tx, H, HD).transpose(0, 2, 1, 3)
        k = jnp.einsum('btd,od->bto', x, Wk).reshape(Bx, Tx, G, HD).transpose(0, 2, 1, 3)
        v = jnp.einsum('btd,od->bto', x, Wv).reshape(Bx, Tx, G, HD).transpose(0, 2, 1, 3)
        q = _rms(q, q_norm_scale)
        k = _rms(k, k_norm_scale)
        pos = kv_lens[:, None] + jnp.arange(Tx, dtype=jnp.int32)
        q = _rope(q, pos)
        k = _rope(k, pos)
        slot = pos // BLOCK
        off = pos % BLOCK
        blk = jnp.take_along_axis(block_tables, slot, axis=1)
        k_blocks = k_blocks.at[blk, :, off, :].set(k.transpose(0, 2, 1, 3))
        v_blocks = v_blocks.at[blk, :, off, :].set(v.transpose(0, 2, 1, 3))
        k_all = k_blocks[block_tables].transpose(0, 2, 1, 3, 4).reshape(Bx, G, -1, HD)
        v_all = v_blocks[block_tables].transpose(0, 2, 1, 3, 4).reshape(Bx, G, -1, HD)
        S = k_all.shape[2]
        qg = q.reshape(Bx, G, GSZ, Tx, HD)
        scores = jnp.einsum('bghtd,bgsd->bghts', qg, k_all) * SCALE
        kpos = jnp.arange(S, dtype=jnp.int32)
        allowed = (kpos[None, None, :] <= pos[:, :, None]) & (kpos[None, None, :] > pos[:, :, None] - WINDOW)
        scores = jnp.where(allowed[:, None, None, :, :], scores, -jnp.inf)
        p = jax.nn.softmax(scores, axis=-1)
        o = jnp.einsum('bghts,bgsd->bghtd', p, v_all).reshape(Bx, H, Tx, HD)
        o = o.transpose(0, 2, 1, 3).reshape(Bx, Tx, H * HD)
        return jnp.einsum('bto,do->btd', o, Wo)
    x = x + _L0_cond_ref(x, itok_B_1_198, L0_cond_weights)
    x = x + _L1_cond_ref(x, L1_cond_Wq, L1_cond_Wk, L1_cond_Wv, L1_cond_Wo, L1_cond_q_norm_scale, L1_cond_k_norm_scale, L1_cond_k_blocks, L1_cond_v_blocks, itok_Bx257_0_4111, itok_B_37_3939)
    return x

_drawn_inputs = setup_inputs


def setup_inputs(seed=0):
    import zlib

    import numpy as np

    out = dict(_drawn_inputs(seed))
    spreads = {}
    factors = {'L1_cond_Wk': 11.963,
     'L1_cond_q_norm_scale': 28.298,
     'L1_cond_k_norm_scale': 64.0,
     'L1_cond_k_blocks': 2.777}
    for name, (base, spread) in spreads.items():
        noise = np.random.default_rng([zlib.crc32(name.encode()), seed]).standard_normal(out[name].shape)
        drawn = base * np.exp(spread * noise) if base else spread * noise
        out[name] = jnp.asarray(drawn.astype(out[name].dtype))
    for name, factor in factors.items():
        out[name] = (out[name] * factor).astype(out[name].dtype)
    return out
```

```python
from contextlib import ExitStack

import numpy as np

import concourse.bass as bass
from concourse import mybir

P = 128
B, C, T = 32, 32, 256
S = 200
H, G, HD = 8, 4, 32
H2 = H // G
BLOCK, WINDOW, NBLK = 16, 128, 257
NPHYS = 16 * NBLK
THETA, EPS = 10000.0, 1e-06
SCALE = 256.0 ** -0.5
QB = P // C
NQ = B // QB
ROWS = B * C
KEYS = WINDOW + C
SLOTS = 11
EN = 3
QUAD = 32
OFFS = BLOCK // 4
NHK = H + G
GROUP = 4
NO_WINNER = 4096
NEG = -1e30
PI = float(np.float32(np.pi))
INV_2PI = float(np.float32(1 / (2 * np.pi)))
MAGIC = 1.5 * 2.0 ** 23

F32 = mybir.dt.float32
F16 = mybir.dt.float16
BF16 = mybir.dt.bfloat16
I32 = mybir.dt.int32
ALU = mybir.AluOpType
ACT = mybir.ActivationFunctionType
X = mybir.AxisListType.X


def two_pi_parts():
    parts, rest = [], 2 * np.pi
    for _ in range(2):
        scale = 2.0 ** (11 - np.floor(np.log2(rest)))
        part = np.floor(rest * scale) / scale
        parts.append(float(part))
        rest -= part
    return parts + [float(np.float32(rest))]


CONST_COLS = {
    "ident": P,
    "blockones": P,
    "eye32": QUAD,
    "slots": NBLK,
    "slot_off": SLOTS,
    "key_off": SLOTS * BLOCK,
    "new_off": OFFS * EN,
    "order": 1,
    "row_in_tile": 1,
    "inv_freq": HD // 2,
}


def const_slices():
    out, at = {}, 0
    for name, n in CONST_COLS.items():
        out[name] = slice(at, at + n)
        at += n
    return out, at


def constants():
    where, width = const_slices()
    c = np.zeros((P, width), np.float32)
    p = np.arange(P)
    c[:, where["ident"]] = np.eye(P)
    c[:, where["blockones"]] = (p[:, None] // QUAD == p[None, :] // QUAD)
    c[:, where["eye32"]] = (p[:, None] % QUAD == np.arange(QUAD)[None, :])
    c[:, where["slots"]] = np.arange(NBLK)
    c[:, where["slot_off"]] = np.arange(SLOTS) - WINDOW // BLOCK
    c[:, where["key_off"]] = np.arange(SLOTS * BLOCK) % BLOCK
    o, e = np.meshgrid(np.arange(OFFS), np.arange(EN), indexing="ij")
    c[:, where["new_off"]] = (BLOCK * e + o).reshape(1, -1) + OFFS * (p[:, None] // QUAD)
    c[:, where["order"]] = C * (p[:, None] % QUAD) + 1
    c[:, where["row_in_tile"]] = p[:, None] % QUAD
    half = HD // 2
    c[:, where["inv_freq"]] = np.float32(1) / np.float32(THETA) ** (np.arange(half, dtype=np.float32) / half)
    return c


def mask_constants():
    left = np.zeros((P, P), np.float32)
    left[:C] = np.tile(np.eye(C), (1, P // C))
    left[C] = 1
    t, i = np.arange(C)[:, None], np.arange(KEYS)[None, :]
    band = np.where((i >= t) & (i <= t + WINDOW - 1), 0.0, NEG)
    return left, band


def build(nc, x, cond, kv_len, tables, cond_w, w_qkv, w_o, q_scale, k_scale, kv_rows,
          consts, mask_left, mask_band, bit_values, out, new_rows, dyn_mask_dram):
    where, width = const_slices()
    C1, C2, C3 = two_pi_parts()
    with ExitStack() as ctx:
        def sb(name, shape, dt=F32):
            return ctx.enter_context(nc.sbuf_tensor(name, shape, dt))

        def sem(name):
            return ctx.enter_context(nc.semaphore(name))

        cst = sb("cst", [P, width])
        ident = cst[:, where["ident"]]
        eye32 = cst[:, where["eye32"]]
        maskL = sb("maskL", [P, P], BF16)
        maskR = sb("maskR", [P, B, KEYS], BF16)
        bits = sb("bits", [P, 4], I32)
        cond_row = sb("cond_row", [P, B], I32)
        kv_row = sb("kv_row", [P, B], I32)
        kv_col = sb("kv_col", [P, 1], I32)
        tab = sb("tab", [P, NBLK], I32)
        x_sb = sb("x_sb", [P, NQ, T])
        wqkv_sb = sb("wqkv_sb", [P, 2, 512])
        wo_sb = sb("wo_sb", [P, 2, T])
        nscale = sb("nscale", [P, 2, HD])
        cond_col = sb("cond_col", [B, 1], I32)
        wsel = sb("wsel", [B, C * C])
        wcd = sb("wcd", [P, NQ, C])
        wbd = sb("wbd", [P, NQ, P])

        kvi = sb("kvi", [P, 2], I32)
        kvs = sb("kvs", [P, 2], I32)
        kva = sb("kva", [P, 2], I32)
        kvf = sb("kvf", [P, 4])
        bitf_i = sb("bitf_i", [P, 4], I32)
        bitf = sb("bitf", [P, 4])
        slot_at = sb("slot_at", [P, SLOTS])
        tabf = sb("tabf", [P, NBLK])
        hit = sb("hit", [P, SLOTS, NBLK])
        blk = sb("blk", [P, SLOTS])
        wrap = sb("wrap", [P, 1])
        dblk = sb("dblk", [P, EN])
        WM = sb("WM", [P, OFFS * EN + EN])
        tnew = sb("tnew", [P, OFFS * EN])
        tge = sb("tge", [P, OFFS * EN])
        tin = sb("tin", [P, OFFS * EN])
        spread = sb("spread", [P, OFFS * EN + EN, QUAD])
        order_b = sb("order_b", [P, OFFS, EN * QUAD], F16)
        entry_b = sb("entry_b", [P, EN * QUAD])
        same = sb("same", [P, SLOTS, EN * QUAD], F16)
        cand = sb("cand", [P, SLOTS, OFFS, EN * QUAD], F16)
        win = sb("win", [P, SLOTS, OFFS])
        wkey = sb("wkey", [B, SLOTS * BLOCK])
        wnone = sb("wnone", [B, SLOTS * BLOCK])
        crow = sb("crow", [B, SLOTS * BLOCK])
        dshift = sb("dshift", [B, SLOTS * BLOCK])
        dmask = sb("dmask", [B, KEYS], BF16)
        lack = sb("lack", [B, 1])
        idx_cache = sb("idx_cache", [P, B], I32)
        idx_new = sb("idx_new", [P, B], I32)
        idx_tail = sb("idx_tail", [P, NQ], I32)

        posf = sb("posf", [P, NQ])
        ang = sb("ang", [P, 2, NQ, HD // 2])
        turns = sb("turns", [P, 2, NQ, HD // 2])
        trig = sb("trig", [P, 2, NQ, HD // 2])
        w1p = sb("w1p", [P, 2, HD])
        wneg = sb("wneg", [P, 2, HD // 2])
        cosw = sb("cosw", [P, 2, NQ, HD])
        sinw = sb("sinw", [P, 2, NQ, HD])

        x1 = sb("x1", [P, NQ, T])
        x1T = sb("x1T", [P, 2, 2, P])
        raw = sb("raw", [P, NQ, NHK * HD])
        sq = sb("sq", [P, 2, NHK, HD])
        ss = sb("ss", [P, NQ, NHK])
        ms = sb("ms", [P, NQ, NHK])
        rms = sb("rms", [P, NQ, NHK])
        rk1 = sb("rk1", [P, GROUP, G, HD])
        rk2 = sb("rk2", [P, GROUP, G, HD])
        rkd = sb("rkd", [P, NQ, G, HD])
        newkv = sb("newkv", [P, NQ, 2 * G * HD])
        rq1 = sb("rq1", [P, H, HD])
        rq2 = sb("rq2", [P, H, HD])
        rqd = sb("rqd", [P, H, HD])
        qrows = sb("qrows", [P, 2, H * HD])

        KV1 = sb("KV1", [P, B, 2 * G * HD])
        KV2 = sb("KV2", [P, NQ, 2 * G * HD])
        qbd = sb("qbd", [P, 2, QB, G, H2 * C])
        KT = sb("KT", [P, 2, QB, KEYS])
        nmax = sb("nmax", [P, B, 2])
        psum_e = sb("psum_e", [P, B, 2])
        rsum = sb("rsum", [P, B, 2])
        Pm = sb("Pm", [P, 2, 2, QB, KEYS])
        Ptail = sb("Ptail", [P, 2, 2, QB, KEYS - WINDOW])
        PT1 = sb("PT1", [P, 2, QB, 2 * P])
        PT2 = sb("PT2", [P, 2, G, QB, H2 * C])
        oT = sb("oT", [P, 2, H2, P])

        bank = [ctx.enter_context(nc.psum_tensor(f"bank{i}", [P, 512], F32)) for i in range(8)]
        ps_x1 = [bank[0], bank[1]]
        ps_x1T = [bank[2], bank[3]]
        ps_qkv = [bank[4], bank[5]]
        ps_entry = bank[6]
        ps_idx = bank[7]
        ps_S = [bank[i][:, 0:2 * KEYS].rearrange("p (h i) -> p h i", h=2) for i in range(3)]
        ps_KT = bank[3]
        ps_PT = [bank[4], bank[5]]
        ps_Q = bank[6][:, 0:256]
        ps_KT2 = bank[6][:, 256:256 + P]
        ps_PT2 = bank[7][:, 0:256]
        ps_oT = bank[7][:, 0:256]
        ps_y = bank[7][:, 0:256]

        l_cond, l_condcol, l_kv, l_tab, l_cst, l_x, l_wqkv, l_wo, l_scale, l_mask = (
            sem(n) for n in ("l_cond", "l_condcol", "l_kv", "l_tab", "l_cst", "l_x", "l_wqkv", "l_wo",
                             "l_scale", "l_mask"))
        wsel_here = sem("wsel_here")
        wcd_here = sem("wcd_here")
        wbd_zero = sem("wbd_zero")
        wbd_done = sem("wbd_done")
        qbd_zero = sem("qbd_zero")
        mask_zero = sem("mask_zero")
        pt2_zero = sem("pt2_zero")
        dve_own = sem("dve_own")
        x1_ps = sem("x1_ps")
        x1_done = sem("x1_done")
        x1T_ps = sem("x1T_ps")
        x1T_done = sem("x1T_done")
        qkv_ps = sem("qkv_ps")
        raw_done = sem("raw_done")
        sq_done = sem("sq_done")
        ss_done = sem("ss_done")
        trig_arg = sem("trig_arg")
        trig_done = sem("trig_done")
        ms_done = sem("ms_done")
        rms_done = sem("rms_done")
        newk_done = sem("newk_done")
        newv_done = sem("newv_done")
        spread_done = sem("spread_done")
        entry_ps = sem("entry_ps")
        entry_done = sem("entry_done")
        crow_done = sem("crow_done")
        wkey_done = sem("wkey_done")
        idx_ps = sem("idx_ps")
        idx_cache_done = sem("idx_cache_done")
        idx_new_done = sem("idx_new_done")
        dmask_done = sem("dmask_done")
        dmask_stored = sem("dmask_stored")
        dmask_here = sem("dmask_here")
        rows_stored = [sem(f"rows_stored{g}") for g in range(NQ // GROUP)]
        cache_here = [sem(f"cache_here{q}") for q in range(NQ)]
        keys_here = [sem(f"keys_here{q}") for q in range(NQ)]
        qrow_done = sem("qrow_done")
        q_ps = sem("q_ps")
        qbd_done = sem("qbd_done")
        kt_ps = sem("kt_ps")
        kt_done = sem("kt_done")
        score_ps = sem("score_ps")
        max_done = sem("max_done")
        exp_done = sem("exp_done")
        norm_done = sem("norm_done")
        tail_done = sem("tail_done")
        pt_ps = sem("pt_ps")
        pt_done = sem("pt_done")
        pt2_ps = sem("pt2_ps")
        pt2_done = sem("pt2_done")
        ot_ps = sem("ot_ps")
        ot_done = sem("ot_done")
        y_ps = sem("y_ps")
        y_done = sem("y_done")
        y_stored = sem("y_stored")

        def every_partition(row, n):
            return row.rearrange("(a n) -> a n", a=1).to_broadcast([P, n])

        block = ctx.enter_context(nc.Block())

        @block.sync
        def _(sp):
            sp.dma_start(cond_col[:, :], cond.rearrange("(b a) -> b a", a=1)).then_inc(l_condcol, 16)
            for c in range(4):
                quadrant = slice(QUAD * c, QUAD * (c + 1))
                sp.dma_start(kv_col[quadrant, :], kv_len.rearrange("(b a) -> b a", a=1)).then_inc(l_kv, 16)
                sp.dma_start(tab[quadrant, :], tables).then_inc(l_tab, 16)
            sp.dma_start(bits[:, :], bit_values).then_inc(l_tab, 16)
            sp.dma_start(x_sb[:, :, :], x.rearrange("(j p) f -> p j f", p=P)).then_inc(l_x, 16)
            sp.dma_start(wqkv_sb[:, :, :], w_qkv.rearrange("(k p) n -> p k n", p=P)).then_inc(l_wqkv, 16)
            sp.wait_ge(wsel_here, 16)
            for j in range(NQ):
                sp.dma_start(wcd[:, j, :],
                             wsel[QB * j:QB * (j + 1), :].rearrange("b (c d) -> b c d", c=C)).then_inc(wcd_here, 16)
            sp.dma_start(wo_sb[:, :, :], w_o.rearrange("(k p) n -> p k n", p=P)).then_inc(l_wo, 16)
            sp.dma_start(maskL[:, :], mask_left).then_inc(l_mask, 16)
            sp.wait_ge(mask_zero, 1)
            sp.dma_start(maskR[0:C, :, :], mask_band.rearrange("t (a i) -> t a i", a=1).to_broadcast([C, B, KEYS])
                         ).then_inc(l_mask, 16)
            sp.wait_ge(dmask_done, 1)
            sp.dma_start(dyn_mask_dram, dmask[:, :]).then_inc(dmask_stored, 16)
            sp.wait_ge(dmask_stored, 16)
            sp.dma_start(maskR[C:C + 1, :, :], dyn_mask_dram.rearrange("(a b) i -> a b i", a=1)
                         ).then_inc(dmask_here, 16)
            rows = new_rows.rearrange("(j p) f -> p j f", p=P)
            for g in range(NQ // GROUP):
                tiles = slice(GROUP * g, GROUP * (g + 1))
                sp.wait_ge(newk_done, g + 1)
                sp.wait_ge(newv_done, GROUP * (g + 1))
                sp.dma_start(rows[:, tiles, :], newkv[:, tiles, :]).then_inc(rows_stored[g], 16)
            out_rows = out.rearrange("(j p) f -> p j f", p=P)
            for q in range(NQ):
                sp.wait_ge(y_done, q + 1)
                sp.dma_start(out_rows[:, q, :], x1[:, q, :]).then_inc(y_stored, 16)
            sp.wait_ge(y_stored, 16 * NQ)

        @block.gpsimd
        def _(pool):
            pool.wait_ge(l_condcol, 16)
            pool.indirect_dma_start(wsel[:, :], None, cond_w,
                                    bass.IndirectOffsetOnAxis(ap=cond_col[:, 0:1], axis=0),
                                    bounds_check=S - 1, oob_is_err=False).then_inc(wsel_here, 16)
            nc.gpsimd.memset(wbd[:, :, :], 0.0).then_inc(wbd_zero, 1)
            nc.gpsimd.memset(maskR[:, :, :], 0.0).then_inc(mask_zero, 1)
            nc.gpsimd.memset(qbd[:, :, :, :, :], 0.0).then_inc(qbd_zero, 1)
            nc.gpsimd.memset(PT2[:, :, :, :, :], 0.0).then_inc(pt2_zero, 1)
            pool.wait_ge(idx_cache_done, 1)
            for b in range(B):
                pool.indirect_dma_start(KV1[:, b, :], None, kv_rows,
                                        bass.IndirectOffsetOnAxis(ap=idx_cache[:, b:b + 1], axis=0),
                                        bounds_check=NPHYS * BLOCK - 1, oob_is_err=False
                                        ).then_inc(cache_here[b // QB], 16)
            pool.wait_ge(idx_new_done, 5)
            for g in range(NQ // GROUP):
                pool.wait_ge(rows_stored[g], 16)
            for q in range(NQ):
                pool.indirect_dma_start(KV2[:, q, :], None, new_rows,
                                        bass.IndirectOffsetOnAxis(ap=idx_tail[:, q:q + 1], axis=0),
                                        bounds_check=ROWS - 1, oob_is_err=False).then_inc(keys_here[q], 16)
                pool.wait_ge(cache_here[q], 16 * QB)
                for b in range(QB * q, QB * (q + 1)):
                    pool.indirect_dma_start(KV1[:, b, :], None, new_rows,
                                            bass.IndirectOffsetOnAxis(ap=idx_new[:, b:b + 1], axis=0),
                                            bounds_check=ROWS - 1, oob_is_err=False).then_inc(keys_here[q], 16)

        @block.scalar
        def _(act):
            act.dma_start(cond_row[:, :], every_partition(cond, B)).then_inc(l_cond, 16)
            act.dma_start(kv_row[:, :], every_partition(kv_len, B)).then_inc(l_cond, 16)
            act.dma_start(cst[:, :], consts).then_inc(l_cst, 16)
            act.dma_start(nscale[:, 0, :], every_partition(q_scale, HD)).then_inc(l_scale, 16)
            act.dma_start(nscale[:, 1, :], every_partition(k_scale, HD)).then_inc(l_scale, 16)
            act.wait_ge(trig_arg, 1)
            nc.scalar.activation(trig[:, :, :, :], ang[:, :, :, :], ACT.Sin).then_inc(trig_done, 1)

            def copy_x1T(j):
                act.wait_ge(x1T_ps, j + 1)
                if j >= 2:
                    act.wait_ge(qkv_ps, j - 1)
                nc.scalar.copy(x1T[:, j % 2, :, :], ps_x1T[j % 2][:, 0:2 * P].rearrange("p (k m) -> p k m", k=2)
                               ).then_inc(x1T_done, 1)

            def split_qkv(j):
                act.wait_ge(qkv_ps, j + 1)
                nc.scalar.copy(raw[:, j, :], ps_qkv[j % 2][:, 0:NHK * HD]).then_inc(raw_done, 1)
                if j >= 2:
                    act.wait_ge(ss_done, j - 1)
                nc.scalar.activation(sq[:, j % 2, :, :],
                                     ps_qkv[j % 2][:, 0:NHK * HD].rearrange("p (h d) -> p h d", d=HD),
                                     ACT.Square).then_inc(sq_done, 1)
                nc.scalar.copy(newkv[:, j, G * HD:], ps_qkv[j % 2][:, NHK * HD:]).then_inc(newv_done, 1)

            def root(g):
                act.wait_ge(ms_done, g + 1)
                tiles = slice(GROUP * g, GROUP * (g + 1))
                nc.scalar.activation(rms[:, tiles, :], ms[:, tiles, :], ACT.Sqrt).then_inc(rms_done, 1)

            copy_x1T(0)
            for j in range(NQ):
                if j + 1 < NQ:
                    copy_x1T(j + 1)
                split_qkv(j)
                if j == 0:
                    act.wait_ge(entry_ps, 1)
                    n = OFFS * EN * QUAD
                    nc.scalar.copy(order_b[:, :, :], ps_entry[:, 0:n].rearrange("p (o e) -> p o e", o=OFFS)
                                   ).then_inc(entry_done, 1)
                    nc.scalar.copy(entry_b[:, :], ps_entry[:, n:n + EN * QUAD]).then_inc(entry_done, 1)
            for g in range(NQ // GROUP):
                root(g)

            def place_q(q):
                act.wait_ge(kt_ps, q + 1)
                if q == 0:
                    act.wait_ge(qbd_zero, 1)
                if q >= 2:
                    act.wait_ge(score_ps, QB * (q - 1))
                for g in range(G):
                    rows = slice(QUAD * g, QUAD * (g + 1))
                    nc.scalar.copy(
                        qbd[rows, q % 2, :, g, :].rearrange("p b (h t) -> p b h t", h=H2),
                        ps_Q[rows, :].rearrange("p (h b t) -> p b h t", h=H2, b=QB)).then_inc(qbd_done, 1)

            def place_k(q):
                act.wait_ge(kt_ps, q + 1)
                if q >= 2:
                    act.wait_ge(score_ps, QB * (q - 1))
                nc.scalar.copy(KT[:, q % 2, :, 0:WINDOW], ps_KT[:, :].rearrange("p (b i) -> p b i", b=QB)
                               ).then_inc(kt_done, 1)
                nc.scalar.copy(KT[:, q % 2, :, WINDOW:], ps_KT2.rearrange("p (b i) -> p b i", b=QB)
                               ).then_inc(kt_done, 1)

            def exps(n):
                q, i = divmod(n, QB)
                act.wait_ge(max_done, n + 1)
                if q >= 2 and i == 0:
                    act.wait_ge(pt_ps, 2 * (q - 1))
                    act.wait_ge(tail_done, q - 1)
                for half in range(2):
                    nc.scalar.activation(Pm[:, q % 2, half, i, :],
                                         ps_S[n % 3][:, half, :], ACT.Exp,
                                         bias=nmax[:, n, half:half + 1],
                                         accum_out=psum_e[:, n, half:half + 1]).then_inc(exp_done, 1)

            def copy_pt(q, pair):
                act.wait_ge(pt_ps, 2 * q + pair + 1)
                if q >= 2:
                    act.wait_ge(ot_ps, q - 1)
                nc.scalar.copy(PT1[:, q % 2, 2 * pair:2 * pair + 2, :],
                               ps_PT[pair][:, :].rearrange("p (b n) -> p b n", b=2)).then_inc(pt_done, 1)

            def copy_ot(q):
                act.wait_ge(ot_ps, q + 1)
                if q >= 2:
                    act.wait_ge(y_ps, q - 1)
                nc.scalar.copy(oT[:, q % 2, :, :].rearrange("p h (b t) -> p b h t", b=QB),
                               ps_oT.rearrange("p (b h t) -> p b h t", b=QB, h=H2)).then_inc(ot_done, 1)

            place_q(0)
            place_k(0)
            for q in range(NQ + 1):
                if q < NQ:
                    exps(QB * q)
                    exps(QB * q + 1)
                if q >= 2:
                    copy_ot(q - 2)
                if q >= 1:
                    copy_pt(q - 1, 0)
                if q < NQ:
                    exps(QB * q + 2)
                    exps(QB * q + 3)
                if q + 1 < NQ:
                    place_q(q + 1)
                    place_k(q + 1)
            copy_ot(NQ - 1)

        @block.vector
        def _(dve):
            steps = [0]

            def link(ins):
                steps[0] += 1
                ins.then_inc(dve_own, 1)
                dve.wait_ge(dve_own, steps[0])

            dve.wait_ge(l_kv, 16 * 4)
            link(nc.vector.tensor_copy(kvi[:, 0:1], kv_col[:, :]))
            link(nc.vector.tensor_scalar(kvi[:, 1:2], kv_col[:, :], 1.0, None, ALU.add))
            dve.wait_ge(l_tab, 16 * 5)
            dve.wait_ge(l_cst, 16)
            nc.vector.tensor_scalar(kvs[:, :], kvi[:, :], 4, None, ALU.arith_shift_right).then_inc(dve_own, 1)
            nc.vector.tensor_scalar(kva[:, :], kvi[:, :], BLOCK - 1, None, ALU.bitwise_and).then_inc(dve_own, 1)
            steps[0] += 2
            link(nc.vector.tensor_copy(tabf[:, :], tab[:, :]))
            nc.vector.tensor_copy(kvf[:, 0:2], kvs[:, :]).then_inc(dve_own, 1)
            nc.vector.tensor_copy(kvf[:, 2:4], kva[:, :]).then_inc(dve_own, 1)
            nc.vector.tensor_tensor(bitf_i[:, :], kva[:, 1:2].to_broadcast([P, 4]), bits[:, :],
                                    ALU.bitwise_and).then_inc(dve_own, 1)
            steps[0] += 3
            dve.wait_ge(dve_own, steps[0])
            nc.vector.tensor_scalar(bitf[:, :], bitf_i[:, :], 0.0, None, ALU.is_gt).then_inc(dve_own, 1)
            steps[0] += 1
            link(nc.vector.tensor_scalar(slot_at[:, :], cst[:, where["slot_off"]], kvf[:, 1:2], None, ALU.add))
            for s in range(SLOTS):
                nc.vector.scalar_tensor_tensor(hit[:, s, :], cst[:, where["slots"]], slot_at[:, s:s + 1],
                                               tabf[:, :], ALU.is_equal, ALU.mult,
                                               accum_out=blk[:, s:s + 1]).then_inc(dve_own, 1)
                steps[0] += 1
            dve.wait_ge(dve_own, steps[0])

            def align(rows, done):
                n = SLOTS * BLOCK
                for k, by in enumerate((8, 4, 2, 1)):
                    n -= by
                    link(nc.vector.tensor_tensor(dshift[:, 0:n], rows[:, by:by + n], rows[:, 0:n], ALU.subtract))
                    ins = nc.vector.scalar_tensor_tensor(rows[:, 0:n], dshift[:, 0:n], bitf[0:B, k:k + 1],
                                                         rows[:, 0:n], ALU.mult, ALU.add)
                    if k < 3:
                        link(ins)
                    else:
                        ins.then_inc(done, 1)

            link(nc.vector.scalar_tensor_tensor(
                crow[:, :].rearrange("b (s o) -> b s o", o=BLOCK),
                blk[0:B, :].rearrange("b (s a) -> b s a", a=1).to_broadcast([B, SLOTS, BLOCK]), float(BLOCK),
                cst[0:B, where["key_off"]].rearrange("b (s o) -> b s o", o=BLOCK), ALU.mult, ALU.add))
            align(crow, crow_done)

            dve.wait_ge(wcd_here, 16 * NQ)
            dve.wait_ge(wbd_zero, 1)
            for c in range(QB):
                rows = slice(QUAD * c, QUAD * (c + 1))
                nc.vector.tensor_copy(wbd[rows, :, QUAD * c:QUAD * (c + 1)], wcd[rows, :, :]).then_inc(wbd_done, 1)

            link(nc.vector.tensor_tensor(wrap[:, :], kvf[:, 1:2], kvf[:, 0:1], ALU.subtract))
            nc.vector.tensor_scalar(tnew[:, :], cst[:, where["new_off"]], kvf[:, 2:3], None,
                                    ALU.subtract).then_inc(dve_own, 1)
            steps[0] += 1
            link(nc.vector.tensor_tensor(dblk[:, :], blk[:, 7:7 + EN], blk[:, 8:8 + EN], ALU.subtract))
            nc.vector.scalar_tensor_tensor(WM[:, OFFS * EN:], dblk[:, :], wrap[:, 0:1], blk[:, 8:8 + EN],
                                           ALU.mult, ALU.add).then_inc(dve_own, 1)
            steps[0] += 1
            link(nc.vector.tensor_scalar(tge[:, :], tnew[:, :], 0.0, None, ALU.is_ge))
            link(nc.vector.scalar_tensor_tensor(tin[:, :], tnew[:, :], float(C - 1), tge[:, :],
                                                ALU.is_le, ALU.mult))
            link(nc.vector.scalar_tensor_tensor(WM[:, 0:OFFS * EN], tnew[:, :], cst[:, where["order"]], tin[:, :],
                                                ALU.add, ALU.mult))
            nw = OFFS * EN + EN
            nc.vector.tensor_tensor(
                spread[:, :, :], WM[:, :].rearrange("p (w a) -> p w a", a=1).to_broadcast([P, nw, QUAD]),
                eye32.rearrange("p (a n) -> p a n", a=1).to_broadcast([P, nw, QUAD]), ALU.mult
            ).then_inc(spread_done, 1)

            dve.wait_ge(idx_ps, 1)
            nc.vector.tensor_copy(idx_cache[:, :], ps_idx[:, 0:B]).then_inc(idx_cache_done, 1)

            def x1_row(j):
                dve.wait_ge(x1_ps, j + 1)
                nc.vector.tensor_tensor(x1[:, j, :], ps_x1[j % 2][:, 0:T], x_sb[:, j, :], ALU.add).then_inc(x1_done, 1)

            dve.wait_ge(l_x, 16)
            x1_row(0)
            x1_row(1)

            dve.wait_ge(l_cond, 32)
            for c in range(QB):
                rows = slice(QUAD * c, QUAD * (c + 1))
                ins = nc.vector.tensor_scalar(posf[rows, :], kv_row[rows, c:B:QB],
                                              cst[rows, where["row_in_tile"]], None, ALU.add)
                ins.then_inc(dve_own, 1)
                steps[0] += 1
            dve.wait_ge(dve_own, steps[0])
            nh = HD // 2
            for part in range(2):
                nc.vector.tensor_tensor(
                    ang[:, part, :, :], posf[:, :].rearrange("p (j a) -> p j a", a=1).to_broadcast([P, NQ, nh]),
                    cst[:, where["inv_freq"]].rearrange("p (a f) -> p a f", a=1).to_broadcast([P, NQ, nh]),
                    ALU.mult).then_inc(dve_own, 1)
                steps[0] += 1
            dve.wait_ge(dve_own, steps[0])
            link(nc.vector.tensor_scalar(turns[:, 0, :, :], ang[:, 0, :, :], INV_2PI, None, ALU.mult))
            link(nc.vector.tensor_scalar(turns[:, 1, :, :], turns[:, 0, :, :], 0.25, MAGIC, ALU.add, ALU.add))
            link(nc.vector.tensor_scalar(turns[:, 0, :, :], turns[:, 0, :, :], MAGIC, None, ALU.add))
            link(nc.vector.tensor_scalar(turns[:, :, :, :], turns[:, :, :, :], MAGIC, None, ALU.subtract))
            for part in (C1, C2, C3):
                link(nc.vector.scalar_tensor_tensor(ang[:, :, :, :], turns[:, :, :, :], -part, ang[:, :, :, :],
                                                    ALU.mult, ALU.add))
            link(nc.vector.tensor_scalar(ang[:, 1, :, :], ang[:, 1, :, :], PI / 2, None, ALU.add))
            nc.vector.tensor_scalar(ang[:, :, :, :], ang[:, :, :, :], PI, -PI, ALU.min, ALU.max).then_inc(trig_arg, 1)

            x1_row(2)
            x1_row(3)

            dve.wait_ge(l_scale, 32)
            link(nc.vector.tensor_scalar(w1p[:, :, :], nscale[:, :, :], 1.0, None, ALU.add))
            link(nc.vector.tensor_scalar(w1p[:, 0, :], w1p[:, 0, :], SCALE, None, ALU.mult))
            link(nc.vector.tensor_scalar(wneg[:, :, :], w1p[:, :, nh:], -1.0, None, ALU.mult))
            dve.wait_ge(trig_done, 1)

            def per_tile(w):
                return w.rearrange("p (a f) -> p a f", a=1).to_broadcast([P, NQ, nh])

            for part in range(2):
                for lo in (0, nh):
                    nc.vector.tensor_tensor(cosw[:, part, :, lo:lo + nh], trig[:, 1, :, :],
                                            per_tile(w1p[:, part, lo:lo + nh]), ALU.mult).then_inc(dve_own, 1)
                nc.vector.tensor_tensor(sinw[:, part, :, 0:nh], trig[:, 0, :, :],
                                        per_tile(wneg[:, part, :]), ALU.mult).then_inc(dve_own, 1)
                nc.vector.tensor_tensor(sinw[:, part, :, nh:], trig[:, 0, :, :],
                                        per_tile(w1p[:, part, 0:nh]), ALU.mult).then_inc(dve_own, 1)
                steps[0] += 4
            dve.wait_ge(dve_own, steps[0])

            def sum_squares(j):
                dve.wait_ge(sq_done, j + 1)
                nc.vector.tensor_reduce(ss[:, j, :], sq[:, j % 2, :, :], X, ALU.add).then_inc(ss_done, 1)

            def mean_squares(g):
                tiles = slice(GROUP * g, GROUP * (g + 1))
                dve.wait_ge(ss_done, GROUP * (g + 1))
                link(nc.vector.tensor_scalar(ms[:, tiles, :], ss[:, tiles, :], 1.0 / HD, EPS, ALU.mult, ALU.add))
                nc.vector.reciprocal(ms[:, tiles, :], ms[:, tiles, :]).then_inc(ms_done, 1)

            def rotate_k(g):
                tiles = slice(GROUP * g, GROUP * (g + 1))
                dve.wait_ge(raw_done, GROUP * (g + 1))
                src = raw[:, tiles, H * HD:].rearrange("p j (h d) -> p j h d", d=HD)

                def table(t, lo, hi):
                    return t[:, 1, tiles, lo:hi].rearrange("p j (a d) -> p j a d", a=1).to_broadcast(
                        [P, GROUP, G, hi - lo])

                nc.vector.tensor_tensor(rk1[:, :, :, :], src, table(cosw, 0, HD), ALU.mult).then_inc(dve_own, 1)
                nc.vector.tensor_tensor(rk2[:, :, :, 0:nh], src[:, :, :, nh:], table(sinw, 0, nh),
                                        ALU.mult).then_inc(dve_own, 1)
                steps[0] += 2
                link(nc.vector.tensor_tensor(rk2[:, :, :, nh:], src[:, :, :, 0:nh], table(sinw, nh, HD), ALU.mult))
                link(nc.vector.tensor_tensor(rkd[:, tiles, :, :], rk1[:, :, :, :], rk2[:, :, :, :], ALU.add))

            def finish_k(g):
                tiles = slice(GROUP * g, GROUP * (g + 1))
                dve.wait_ge(rms_done, g + 1)
                nc.vector.tensor_tensor(
                    newkv[:, tiles, 0:G * HD].rearrange("p j (h d) -> p j h d", d=HD), rkd[:, tiles, :, :],
                    rms[:, tiles, H:].rearrange("p j (h a) -> p j h a", a=1).to_broadcast([P, GROUP, G, HD]),
                    ALU.mult).then_inc(newk_done, 1)

            x1_row(4)
            sum_squares(0)
            x1_row(5)
            sum_squares(1)

            dve.wait_ge(entry_done, 2)
            ne = EN * QUAD
            link(nc.vector.tensor_tensor(
                same[:, :, :], blk[:, :].rearrange("p (s a) -> p s a", a=1).to_broadcast([P, SLOTS, ne]),
                entry_b[:, :].rearrange("p (a e) -> p a e", a=1).to_broadcast([P, SLOTS, ne]), ALU.is_equal))
            x1_row(6)
            sum_squares(2)
            link(nc.vector.tensor_tensor(
                cand[:, :, :, :],
                same[:, :, :].rearrange("p s (a e) -> p s a e", a=1).to_broadcast([P, SLOTS, OFFS, ne]),
                order_b[:, :, :].rearrange("p (a o) e -> p a o e", a=1).to_broadcast([P, SLOTS, OFFS, ne]),
                ALU.mult))
            x1_row(7)
            sum_squares(3)
            link(nc.vector.tensor_reduce(win[:, :, :], cand[:, :, :, :], X, ALU.max))
            mean_squares(0)
            rotate_k(0)
            sum_squares(4)
            for c in range(4):
                nc.vector.tensor_copy(
                    wkey[:, :].rearrange("b (s c o) -> b s c o", c=4, o=OFFS)[:, :, c, :],
                    win[QUAD * c:QUAD * (c + 1), :, :]).then_inc(dve_own, 1)
                steps[0] += 1
            dve.wait_ge(dve_own, steps[0])
            link(nc.vector.tensor_scalar(wnone[:, :], wkey[:, :], 0.0, float(NO_WINNER), ALU.is_equal, ALU.mult))
            link(nc.vector.scalar_tensor_tensor(wkey[:, :], wkey[:, :], -1.0, wnone[:, :], ALU.add, ALU.add))
            dve.wait_ge(crow_done, 1)
            align(wkey, wkey_done)
            sum_squares(5)
            link(nc.vector.tensor_scalar(lack[:, :], kv_col[0:B, :], -1.0, float(WINDOW - 1), ALU.mult, ALU.add))
            nc.vector.tensor_scalar(dmask[:, :], cst[0:B, where["slots"]][:, 0:KEYS], lack[:, 0:1], NEG,
                                    ALU.is_lt, ALU.mult).then_inc(dmask_done, 1)
            sum_squares(6)
            dve.wait_ge(idx_ps, 2)
            nc.vector.tensor_copy(idx_new[:, :], ps_idx[:, B:2 * B]).then_inc(idx_new_done, 1)
            for c in range(QB):
                nc.vector.tensor_scalar(idx_tail[QUAD * c:QUAD * (c + 1), :], ps_idx[0:QUAD, 2 * B + c:3 * B:QB],
                                        float(ROWS - 1), None, ALU.min).then_inc(idx_new_done, 1)
            sum_squares(7)
            mean_squares(1)
            rotate_k(1)
            finish_k(0)
            finish_k(1)

            def finish_q(q):
                src = raw[:, q, 0:H * HD].rearrange("p (h d) -> p h d", d=HD)

                def table(t, lo, hi):
                    return t[:, 0, q, lo:hi].rearrange("p (a d) -> p a d", a=1).to_broadcast([P, H, hi - lo])

                if q >= 2:
                    dve.wait_ge(q_ps, q - 1)
                nc.vector.tensor_tensor(rq1[:, :, :], src, table(cosw, 0, HD), ALU.mult).then_inc(dve_own, 1)
                nc.vector.tensor_tensor(rq2[:, :, 0:nh], src[:, :, nh:], table(sinw, 0, nh),
                                        ALU.mult).then_inc(dve_own, 1)
                steps[0] += 2
                link(nc.vector.tensor_tensor(rq2[:, :, nh:], src[:, :, 0:nh], table(sinw, nh, HD), ALU.mult))
                link(nc.vector.tensor_tensor(rqd[:, :, :], rq1[:, :, :], rq2[:, :, :], ALU.add))
                link(nc.vector.tensor_tensor(
                    qrows[:, q % 2, :].rearrange("p (h d) -> p h d", d=HD), rqd[:, :, :],
                    rms[:, q, 0:H].rearrange("p (h a) -> p h a", a=1).to_broadcast([P, H, HD]), ALU.mult))
                nc.vector.sem_inc(qrow_done, 1)

            def row_max(n):
                dve.wait_ge(score_ps, n + 1)
                nc.vector.tensor_reduce(nmax[:, n, :],
                                        ps_S[n % 3], X, ALU.max, negate=True).then_inc(max_done, 1)

            def normalise(n):
                q, i = divmod(n, QB)
                dve.wait_ge(exp_done, 2 * (n + 1))
                link(nc.vector.reciprocal(rsum[:, n, :], psum_e[:, n, :]))
                for half in range(2):
                    nc.vector.tensor_scalar(Pm[:, q % 2, half, i, 0:WINDOW], Pm[:, q % 2, half, i, 0:WINDOW],
                                            rsum[:, n, half:half + 1], None, ALU.mult).then_inc(norm_done, 1)

            def normalise_tails(q):
                if q >= 2:
                    dve.wait_ge(pt2_ps, q - 1)
                nc.vector.tensor_tensor(
                    Ptail[:, q % 2, :, :, :], Pm[:, q % 2, :, :, WINDOW:],
                    rsum[:, QB * q:QB * (q + 1), :].rearrange("p (a b) h -> p h b a", a=1).to_broadcast(
                        [P, 2, QB, KEYS - WINDOW]), ALU.mult).then_inc(tail_done, 1)

            def copy_pt(q, pair):
                dve.wait_ge(pt_ps, 2 * q + pair + 1)
                if q >= 2:
                    dve.wait_ge(ot_ps, q - 1)
                nc.vector.tensor_copy(PT1[:, q % 2, 2 * pair:2 * pair + 2, :],
                                      ps_PT[pair][:, :].rearrange("p (b n) -> p b n", b=2)).then_inc(pt2_done, 1)
                dve.wait_ge(pt2_ps, q + 1)
                if q == 0:
                    dve.wait_ge(pt2_zero, 1)
                for i in range(QB):
                    rows = slice(QUAD * i, QUAD * (i + 1))
                    nc.vector.tensor_copy(PT2[rows, q % 2, :, i, :],
                                          ps_PT2[rows, :].rearrange("p (g m) -> p g m", g=G)).then_inc(pt2_done, 1)

            def finish_y(q):
                dve.wait_ge(y_ps, q + 1)
                nc.vector.tensor_tensor(x1[:, q, :], ps_y, x1[:, q, :], ALU.add).then_inc(y_done, 1)

            finish_q(0)
            finish_q(1)
            for q in range(NQ + 1):
                if q < NQ:
                    row_max(QB * q)
                    row_max(QB * q + 1)
                    normalise(QB * q)
                    normalise(QB * q + 1)
                    row_max(QB * q + 2)
                    row_max(QB * q + 3)
                if q >= 2:
                    finish_y(q - 2)
                if q >= 1:
                    copy_pt(q - 1, 1)
                if q < NQ:
                    normalise(QB * q + 2)
                    normalise(QB * q + 3)
                    normalise_tails(q)
                if q + 2 < NQ:
                    finish_q(q + 2)
            finish_y(NQ - 1)

        @block.tensor
        def _(pe):
            def x1_rows(j):
                if j >= 2:
                    pe.wait_ge(x1_done, j - 1)
                nc.tensor.matmul(ps_x1[j % 2][:, 0:T], wbd[:, j, :], x_sb[:, j, :],
                                 start=True, stop=True).then_inc(x1_ps, 1)

            def x1_columns(j):
                pe.wait_ge(x1_done, j + 1)
                if j >= 2:
                    pe.wait_ge(x1T_done, j - 1)
                for k in range(2):
                    last = nc.tensor.transpose(ps_x1T[j % 2][:, P * k:P * (k + 1)],
                                               x1[:, j, P * k:P * (k + 1)], ident)
                last.then_inc(x1T_ps, 1)

            def project(j):
                pe.wait_ge(x1T_done, j + 1)
                if j >= 2:
                    pe.wait_ge(newv_done, j - 1)
                for k in range(2):
                    last = nc.tensor.matmul(ps_qkv[j % 2][:, :], x1T[:, j % 2, k, :], wqkv_sb[:, k, :],
                                            start=(k == 0), stop=(k == 1))
                last.then_inc(qkv_ps, 1)

            pe.wait_ge(l_cst, 16)
            pe.wait_ge(crow_done, 1)
            nc.tensor.transpose(ps_idx[:, 0:B], crow[:, 0:WINDOW], ident[0:B, 0:B]).then_inc(idx_ps, 1)
            pe.wait_ge(wbd_done, QB)
            pe.wait_ge(l_x, 16)
            pe.wait_ge(l_wqkv, 16)
            x1_rows(0)
            x1_rows(1)
            pe.wait_ge(spread_done, 1)
            nc.tensor.matmul(ps_entry[:, 0:(OFFS * EN + EN) * QUAD], cst[:, where["blockones"]],
                             spread[:, :, :].rearrange("p w n -> p (w n)"), start=True, stop=True
                             ).then_inc(entry_ps, 1)
            x1_columns(0)
            for j in range(NQ):
                if j + 1 < NQ:
                    x1_columns(j + 1)
                if j + 2 < NQ:
                    x1_rows(j + 2)
                project(j)
                if j == 6:
                    pe.wait_ge(wkey_done, 1)
                    pe.wait_ge(idx_cache_done, 1)
                    nc.tensor.transpose(ps_idx[:, B:2 * B], wkey[:, 0:WINDOW], ident[0:B, 0:B])
                    nc.tensor.transpose(ps_idx[0:C, 2 * B:3 * B], wkey[:, WINDOW:KEYS], ident[0:B, 0:B]
                                        ).then_inc(idx_ps, 1)

            def q_columns(q):
                pe.wait_ge(qrow_done, q + 1)
                if q >= 1:
                    pe.wait_ge(qbd_done, G * q)
                    pe.wait_ge(kt_done, 2 * q)
                for h in range(H2):
                    last = nc.tensor.transpose(ps_Q[:, P * h:P * (h + 1)], qrows[:, q % 2, P * h:P * (h + 1)], ident)
                last.then_inc(q_ps, 1)

            def k_columns(q):
                pe.wait_ge(keys_here[q], 16 * (QB + 1))
                if q >= 1:
                    pe.wait_ge(kt_done, 2 * q)
                for i in range(QB):
                    nc.tensor.transpose(ps_KT[:, P * i:P * (i + 1)], KV1[:, QB * q + i, 0:G * HD], ident)
                nc.tensor.transpose(ps_KT2, KV2[:, q, 0:G * HD], ident).then_inc(kt_ps, 1)

            def scores(n):
                q, i = divmod(n, QB)
                if i == 0:
                    pe.wait_ge(qbd_done, G * (q + 1))
                    pe.wait_ge(kt_done, 2 * (q + 1))
                if n == 0:
                    pe.wait_ge(l_mask, 16 * 2)
                    pe.wait_ge(dmask_here, 16)
                if n >= 3:
                    pe.wait_ge(exp_done, 2 * (n - 2))
                nc.tensor.matmul(ps_S[n % 3], maskL[:, :],
                                 maskR[:, n, :].rearrange("p (a i) -> p a i", a=1).to_broadcast([P, 2, KEYS]),
                                 start=True, stop=False, skip_group_check=True)
                for half in range(2):
                    last = nc.tensor.matmul(ps_S[n % 3][:, half, :],
                                            qbd[:, q % 2, i, 2 * half:2 * half + 2, :].rearrange("p g m -> p (g m)"),
                                            KT[:, q % 2, i, :], start=False, stop=True, skip_group_check=True)
                last.then_inc(score_ps, 1)

            def p_columns(q, pair):
                pe.wait_ge(norm_done, 2 * (QB * q + 2 * pair + 2))
                if q >= 1:
                    if pair == 0:
                        pe.wait_ge(pt_done, q)
                    else:
                        pe.wait_ge(pt2_done, (1 + QB) * q)
                for k in range(2):
                    for half in range(2):
                        c = (2 * k + half) * P
                        last = nc.tensor.transpose(ps_PT[pair][:, c:c + P],
                                                   Pm[:, q % 2, half, 2 * pair + k, 0:WINDOW], ident)
                last.then_inc(pt_ps, 1)

            def p_tail_columns(q):
                pe.wait_ge(tail_done, q + 1)
                if q >= 1:
                    pe.wait_ge(y_done, q)
                for half in range(2):
                    last = nc.tensor.transpose(ps_PT2[:, P * half:P * (half + 1)],
                                               Ptail[:, q % 2, half, :, :].rearrange("p b i -> p (b i)"), ident)
                last.then_inc(pt2_ps, 1)

            def values(q, pair):
                if pair == 0:
                    pe.wait_ge(pt_done, q + 1)
                    pe.wait_ge(pt2_done, (1 + QB) * (q + 1))
                    if q >= 1:
                        pe.wait_ge(ot_done, q)
                if pair == 0:
                    for g in range(G):
                        nc.tensor.matmul(ps_oT[QUAD * g:QUAD * (g + 1), :],
                                         KV2[:, q, HD * (G + g):HD * (G + g + 1)],
                                         PT2[:, q % 2, g, :, :].rearrange("p b m -> p (b m)"),
                                         start=True, stop=False, skip_group_check=True)
                for i in (2 * pair, 2 * pair + 1):
                    for g in range(G):
                        last = nc.tensor.matmul(ps_oT[QUAD * g:QUAD * (g + 1), 64 * i:64 * (i + 1)],
                                                KV1[:, QB * q + i, HD * (G + g):HD * (G + g + 1)],
                                                PT1[:, q % 2, i, 64 * g:64 * (g + 1)],
                                                start=False, stop=True, skip_group_check=True)
                if pair == 1:
                    last.then_inc(ot_ps, 1)

            def output(q):
                if q == 0:
                    pe.wait_ge(l_wo, 16)
                pe.wait_ge(ot_done, q + 1)
                if q >= 1:
                    pe.wait_ge(y_done, q)
                for h in range(H2):
                    last = nc.tensor.matmul(ps_y, oT[:, q % 2, h, :], wo_sb[:, h, :], start=(h == 0), stop=(h == 1))
                last.then_inc(y_ps, 1)

            pe.wait_ge(newv_done, NQ)
            pe.wait_ge(idx_new_done, 5)
            pe.wait_ge(entry_done, 2)
            q_columns(0)
            k_columns(0)
            for q in range(NQ + 1):
                if q < NQ:
                    scores(QB * q)
                    scores(QB * q + 1)
                if q >= 1:
                    p_columns(q - 1, 0)
                if q >= 2:
                    output(q - 2)
                if q < NQ:
                    scores(QB * q + 2)
                    scores(QB * q + 3)
                if q >= 1:
                    p_columns(q - 1, 1)
                    p_tail_columns(q - 1)
                if q + 1 < NQ:
                    q_columns(q + 1)
                    k_columns(q + 1)
                if q >= 1:
                    values(q - 1, 0)
                    values(q - 1, 1)
            output(NQ - 1)


def kernel(x, itok_B_1_198, itok_Bx257_0_4111, itok_B_37_3939, L0_cond_weights, L1_cond_Wq, L1_cond_Wk,
           L1_cond_Wv, L1_cond_Wo, L1_cond_q_norm_scale, L1_cond_k_norm_scale, L1_cond_k_blocks,
           L1_cond_v_blocks):
    import concourse.bacc as bacc
    import ml_dtypes
    from concourse.bass_utils import run_bass_kernel_spmd as run

    def q_order(w):
        return np.asarray(w).reshape(G, H2, HD, -1).transpose(1, 0, 2, 3).reshape(H * HD, -1)

    wo_T = np.asarray(L1_cond_Wo).T
    mask_left, mask_band = mask_constants()
    arrays = {
        "x": np.asarray(x).reshape(ROWS, T),
        "cond": np.asarray(itok_B_1_198),
        "kv_len": np.asarray(itok_B_37_3939),
        "tables": np.asarray(itok_Bx257_0_4111),
        "cond_w": np.asarray(L0_cond_weights).reshape(S, C * C),
        "w_qkv": np.concatenate([q_order(L1_cond_Wq).T, np.asarray(L1_cond_Wk).T, np.asarray(L1_cond_Wv).T], axis=1),
        "w_o": q_order(wo_T),
        "q_scale": np.asarray(L1_cond_q_norm_scale),
        "k_scale": np.asarray(L1_cond_k_norm_scale),
        "kv_rows": np.concatenate([np.asarray(a).transpose(0, 2, 1, 3).reshape(NPHYS * BLOCK, G * HD)
                                   for a in (L1_cond_k_blocks, L1_cond_v_blocks)], axis=1),
        "consts": constants(),
        "mask_left": mask_left.astype(ml_dtypes.bfloat16),
        "mask_band": mask_band.astype(ml_dtypes.bfloat16),
        "bit_values": np.tile(np.array([[8, 4, 2, 1]], np.int32), (P, 1)),
    }
    nc = bacc.Bacc("TRN2", target_bir_lowering=False, num_devices=1)
    arrays = {k: np.ascontiguousarray(a) for k, a in arrays.items()}
    aps = [nc.dram_tensor(k, a.shape, mybir.dt.from_np(a.dtype), kind="ExternalInput").ap()
           for k, a in arrays.items()]
    out = nc.dram_tensor("out", (ROWS, T), F32, kind="ExternalOutput").ap()
    new_rows = nc.dram_tensor("new_rows", (ROWS, 2 * G * HD), F32, kind="Internal").ap()
    dyn_mask = nc.dram_tensor("dyn_mask", (B, KEYS), BF16, kind="Internal").ap()
    build(nc, *aps, out, new_rows, dyn_mask)
    r = run(nc, [arrays], core_ids=[0])
    return r.results[0]["out"].reshape(B, C, T)
```

```python
from contextlib import ExitStack

import numpy as np

import concourse.bass as bass
from concourse import mybir

P = 128
B, C, T = 32, 32, 256
S = 200
H, G, HD = 8, 4, 32
H2 = H // G
BLOCK, WINDOW, NBLK = 16, 128, 257
NPHYS = 16 * NBLK
THETA, EPS = 10000.0, 1e-06
SCALE = 256.0 ** -0.5
QB = P // C
NQ = B // QB
ROWS = B * C
KEYS = WINDOW + C
SLOTS = 11
EN = 3
QUAD = 32
OFFS = BLOCK // 4
NHK = H + G
GROUP = 4
Q_GROUPS = [slice(0, 1), slice(1, 4), slice(4, 8)]
NO_WINNER = 4096
NEG = -1e30
PI = float(np.float32(np.pi))
INV_2PI = float(np.float32(1 / (2 * np.pi)))
MAGIC = 1.5 * 2.0 ** 23

F32 = mybir.dt.float32
F16 = mybir.dt.float16
BF16 = mybir.dt.bfloat16
I32 = mybir.dt.int32
ALU = mybir.AluOpType
ACT = mybir.ActivationFunctionType
X = mybir.AxisListType.X


def two_pi_parts():
    parts, rest = [], 2 * np.pi
    for _ in range(2):
        scale = 2.0 ** (11 - np.floor(np.log2(rest)))
        part = np.floor(rest * scale) / scale
        parts.append(float(part))
        rest -= part
    return parts + [float(np.float32(rest))]


CONST_COLS = {
    "ident": P,
    "blockones": P,
    "eye32": QUAD,
    "slots": NBLK,
    "slot_off": SLOTS,
    "key_off": SLOTS * BLOCK,
    "new_off": OFFS * EN,
    "order": 1,
    "row_in_tile": 1,
    "inv_freq": HD // 2,
}


def const_slices():
    out, at = {}, 0
    for name, n in CONST_COLS.items():
        out[name] = slice(at, at + n)
        at += n
    return out, at


def constants():
    where, width = const_slices()
    c = np.zeros((P, width), np.float32)
    p = np.arange(P)
    c[:, where["ident"]] = np.eye(P)
    c[:, where["blockones"]] = (p[:, None] // QUAD == p[None, :] // QUAD)
    c[:, where["eye32"]] = (p[:, None] % QUAD == np.arange(QUAD)[None, :])
    c[:, where["slots"]] = np.arange(NBLK)
    c[:, where["slot_off"]] = np.arange(SLOTS) - WINDOW // BLOCK
    c[:, where["key_off"]] = np.arange(SLOTS * BLOCK) % BLOCK
    o, e = np.meshgrid(np.arange(OFFS), np.arange(EN), indexing="ij")
    c[:, where["new_off"]] = (BLOCK * e + o).reshape(1, -1) + OFFS * (p[:, None] // QUAD)
    c[:, where["order"]] = C * (p[:, None] % QUAD) + 1
    c[:, where["row_in_tile"]] = p[:, None] % QUAD
    half = HD // 2
    c[:, where["inv_freq"]] = np.float32(1) / np.float32(THETA) ** (np.arange(half, dtype=np.float32) / half)
    return c


def mask_constants():
    left = np.zeros((P, P), np.float32)
    left[:C] = np.tile(np.eye(C), (1, P // C))
    left[C] = 1
    t, i = np.arange(C)[:, None], np.arange(KEYS)[None, :]
    band = np.where((i >= t) & (i <= t + WINDOW - 1), 0.0, NEG)
    return left, band


def build(nc, x, cond, kv_len, tables, cond_w, w_qkv, w_o, q_scale, k_scale, kv_rows,
          consts, mask_left, mask_band, bit_values, out, new_rows, dyn_mask_dram):
    where, width = const_slices()
    C1, C2, C3 = two_pi_parts()
    with ExitStack() as ctx:
        def sb(name, shape, dt=F32):
            return ctx.enter_context(nc.sbuf_tensor(name, shape, dt))

        def sem(name):
            return ctx.enter_context(nc.semaphore(name))

        cst = sb("cst", [P, width])
        ident = cst[:, where["ident"]]
        eye32 = cst[:, where["eye32"]]
        maskL = sb("maskL", [P, P], BF16)
        maskR = sb("maskR", [P, B, KEYS], BF16)
        bits = sb("bits", [P, 4], I32)
        kv_row = sb("kv_row", [P, B], I32)
        kv_col = sb("kv_col", [P, 1], I32)
        tab = sb("tab", [P, NBLK], I32)
        x_sb = sb("x_sb", [P, NQ, T])
        wqkv_sb = sb("wqkv_sb", [P, 2, 512])
        wo_sb = sb("wo_sb", [P, 2, T])
        nscale = sb("nscale", [P, 2, HD])
        cond_col = sb("cond_col", [B, 1], I32)
        wsel = sb("wsel", [B, C * C])
        wcd = sb("wcd", [P, NQ, C])
        wbd = sb("wbd", [P, NQ, P])

        kvi = sb("kvi", [P, 2], I32)
        kvs = sb("kvs", [P, 2], I32)
        kva = sb("kva", [P, 2], I32)
        kvf = sb("kvf", [P, 4])
        bitf_i = sb("bitf_i", [P, 4], I32)
        bitf = sb("bitf", [P, 4])
        slot_at = sb("slot_at", [P, SLOTS])
        tabf = sb("tabf", [P, NBLK])
        blk = sb("blk", [P, SLOTS])
        wrap = sb("wrap", [P, 1])
        dblk = sb("dblk", [P, EN])
        WM = sb("WM", [P, OFFS * EN + EN])
        tnew = sb("tnew", [P, OFFS * EN])
        tge = sb("tge", [P, OFFS * EN])
        tin = sb("tin", [P, OFFS * EN])
        spread = sb("spread", [P, OFFS * EN + EN, QUAD])
        order_b = sb("order_b", [P, OFFS, EN * QUAD], F16)
        entry_b = sb("entry_b", [P, EN * QUAD])
        same = sb("same", [P, SLOTS, EN * QUAD], F16)
        cand = sb("cand", [P, SLOTS, OFFS, EN * QUAD], F16)
        win = sb("win", [P, SLOTS, OFFS])
        wkey = sb("wkey", [B, SLOTS * BLOCK])
        wnone = sb("wnone", [B, SLOTS * BLOCK])
        crow = sb("crow", [B, SLOTS * BLOCK])
        dshift = sb("dshift", [B, SLOTS * BLOCK])
        dmask = sb("dmask", [B, KEYS], BF16)
        lack = sb("lack", [B, 1])
        idx_cache = sb("idx_cache", [P, B], I32)
        idx_new = sb("idx_new", [P, B], I32)
        idx_tail = sb("idx_tail", [P, NQ], I32)

        posf = sb("posf", [P, NQ])
        ang = sb("ang", [P, 2, NQ, HD // 2])
        turns = sb("turns", [P, 2, NQ, HD // 2])
        trig = sb("trig", [P, 2, NQ, HD // 2])
        w1p = sb("w1p", [P, 2, HD])
        wneg = sb("wneg", [P, 2, HD // 2])
        cosw = sb("cosw", [P, 2, NQ, HD])
        sinw = sb("sinw", [P, 2, NQ, HD])

        x1 = sb("x1", [P, NQ, T])
        x1T = sb("x1T", [P, 2, 2, P])
        raw = sb("raw", [P, NQ, NHK * HD])
        sq = sb("sq", [P, 4, NHK, HD])
        ss = sb("ss", [P, NQ, NHK])
        ms = sb("ms", [P, NQ, NHK])
        rms = sb("rms", [P, NQ, NHK])
        rk1 = sb("rk1", [P, GROUP, G, HD])
        rk2 = sb("rk2", [P, GROUP, G, HD])
        rkd = sb("rkd", [P, NQ, G, HD])
        newkv = sb("newkv", [P, NQ, 2 * G * HD])
        rq1 = x_sb[:, 0:GROUP, :].rearrange("p j (h d) -> p j h d", d=HD)
        rq2 = x_sb[:, GROUP:2 * GROUP, :].rearrange("p j (h d) -> p j h d", d=HD)
        qrows = sb("qrows", [P, NQ, H * HD])

        KV1 = sb("KV1", [P, B, 2 * G * HD])
        hit = KV1[:, :, :].rearrange("p b n -> p (b n)")[:, 0:SLOTS * NBLK].rearrange("p (s n) -> p s n", s=SLOTS)
        KV2 = sb("KV2", [P, NQ, 2 * G * HD])
        qbd = sb("qbd", [P, 2, QB, G, H2 * C])
        KT = sb("KT", [P, 2, QB, KEYS])
        nmax = sb("nmax", [P, B, 2])
        psum_e = sb("psum_e", [P, B, 2])
        rsum = sb("rsum", [P, B, 2])
        Pm = sb("Pm", [P, 2, 2, QB, KEYS])
        Ptail = sb("Ptail", [P, 2, 2, QB, KEYS - WINDOW])
        PT1 = sb("PT1", [P, 2, QB, 2 * P])
        PT2 = sb("PT2", [P, 2, G, QB, H2 * C])
        oT = sb("oT", [P, 2, H2, P])

        bank = [ctx.enter_context(nc.psum_tensor(f"bank{i}", [P, 512], F32)) for i in range(8)]
        ps_x1 = [bank[0], bank[1]]
        ps_x1T = [bank[2], bank[3]]
        ps_qkv = [bank[4], bank[5]]
        ps_entry = bank[6]
        ps_idx = bank[7]
        ps_S = [bank[i][:, 0:2 * KEYS].rearrange("p (h i) -> p h i", h=2) for i in range(3)]
        ps_KT = bank[3]
        ps_PT = [bank[4], bank[5]]
        ps_Q = bank[6][:, 0:256]
        ps_KT2 = bank[6][:, 256:256 + P]
        ps_PT2 = bank[7][:, 0:256]
        ps_oT = bank[7][:, 0:256]
        ps_y = bank[7][:, 0:256]

        l_kvrow, l_condcol, l_kv, l_tab, l_cst, l_x, l_wqkv, l_wo, l_scale, l_mask = (
            sem(n) for n in ("l_kvrow", "l_condcol", "l_kv", "l_tab", "l_cst", "l_x", "l_wqkv", "l_wo",
                             "l_scale", "l_mask"))
        wsel_here = sem("wsel_here")
        wcd_here = sem("wcd_here")
        wbd_zero = sem("wbd_zero")
        wbd_done = sem("wbd_done")
        qbd_zero = sem("qbd_zero")
        mask_zero = sem("mask_zero")
        pt2_zero = sem("pt2_zero")
        dve_own = sem("dve_own")
        x1_ps = sem("x1_ps")
        x1_done = sem("x1_done")
        x1T_ps = sem("x1T_ps")
        x1T_done = sem("x1T_done")
        qkv_ps = sem("qkv_ps")
        raw_done = sem("raw_done")
        sq_done = sem("sq_done")
        ss_done = sem("ss_done")
        trig_arg = sem("trig_arg")
        trig_done = sem("trig_done")
        ms_done = sem("ms_done")
        rms_done = sem("rms_done")
        newk_done = sem("newk_done")
        newv_done = sem("newv_done")
        spread_done = sem("spread_done")
        entry_ps = sem("entry_ps")
        entry_done = sem("entry_done")
        crow_done = sem("crow_done")
        wkey_done = sem("wkey_done")
        idx_ps = sem("idx_ps")
        idx_cache_done = sem("idx_cache_done")
        idx_new_done = sem("idx_new_done")
        dmask_done = sem("dmask_done")
        dmask_stored = sem("dmask_stored")
        dmask_here = sem("dmask_here")
        rows_stored = [sem(f"rows_stored{g}") for g in range(NQ // GROUP)]
        cache_here = [sem(f"cache_here{q}") for q in range(NQ)]
        keys_here = [sem(f"keys_here{q}") for q in range(NQ)]
        qrow_done = sem("qrow_done")
        q_ps = sem("q_ps")
        qbd_done = sem("qbd_done")
        kt_ps = sem("kt_ps")
        kt_done = sem("kt_done")
        score_ps = sem("score_ps")
        max_done = sem("max_done")
        exp_done = sem("exp_done")
        norm_done = sem("norm_done")
        tail_done = sem("tail_done")
        pt_ps = sem("pt_ps")
        pt_done = sem("pt_done")
        ptb_done = sem("ptb_done")
        ptb2_done = sem("ptb2_done")
        pt2_ps = sem("pt2_ps")
        pt2_done = sem("pt2_done")
        ot_ps = sem("ot_ps")
        ot_done = sem("ot_done")
        y_ps = sem("y_ps")
        y_done = sem("y_done")
        y_stored = sem("y_stored")

        def every_partition(row, n):
            return row.rearrange("(a n) -> a n", a=1).to_broadcast([P, n])

        def four_times(rows):
            return rows.rearrange("(a b) n -> a b n", a=1).to_broadcast([4, B, rows.shape[1]])

        def place_weights(queue, part):
            queue.wait_ge(wsel_here, 16)
            for j in range(part * NQ // 2, (part + 1) * NQ // 2):
                queue.dma_start(wcd[:, j, :], wsel[QB * j:QB * (j + 1), :].rearrange("b (c d) -> b c d", c=C)
                                ).then_inc(wcd_here, 16)

        block = ctx.enter_context(nc.Block())

        @block.sync
        def _(sp):
            sp.dma_start(kv_col[:, :], four_times(kv_len.rearrange("(b a) -> b a", a=1))).then_inc(l_kv, 16)
            sp.dma_start(cond_col[:, :], cond.rearrange("(b a) -> b a", a=1)).then_inc(l_condcol, 16)
            sp.dma_start(bits[:, :], bit_values).then_inc(l_kv, 16)
            sp.dma_start(x_sb[:, :, :], x.rearrange("(j p) f -> p j f", p=P)).then_inc(l_x, 16)
            place_weights(sp, 0)
            sp.dma_start(wqkv_sb[:, :, :], w_qkv.rearrange("(k p) n -> p k n", p=P)).then_inc(l_wqkv, 16)
            sp.dma_start(wo_sb[:, :, :], w_o.rearrange("(k p) n -> p k n", p=P)).then_inc(l_wo, 16)
            sp.dma_start(maskL[:, :], mask_left).then_inc(l_mask, 16)
            sp.wait_ge(mask_zero, 1)
            sp.dma_start(maskR[0:C, :, :], mask_band.rearrange("t (a i) -> t a i", a=1).to_broadcast([C, B, KEYS])
                         ).then_inc(l_mask, 16)
            sp.wait_ge(dmask_done, 1)
            sp.dma_start(dyn_mask_dram, dmask[:, :]).then_inc(dmask_stored, 16)
            sp.wait_ge(dmask_stored, 16)
            sp.dma_start(maskR[C:C + 1, :, :], dyn_mask_dram.rearrange("(a b) i -> a b i", a=1)
                         ).then_inc(dmask_here, 16)
            rows = new_rows.rearrange("(j p) f -> p j f", p=P)
            for g in range(NQ // GROUP):
                tiles = slice(GROUP * g, GROUP * (g + 1))
                sp.wait_ge(newk_done, g + 1)
                sp.wait_ge(newv_done, GROUP * (g + 1))
                sp.dma_start(rows[:, tiles, :], newkv[:, tiles, :]).then_inc(rows_stored[g], 16)
            out_rows = out.rearrange("(j p) f -> p j f", p=P)
            for q in range(NQ):
                sp.wait_ge(y_done, q + 1)
                sp.dma_start(out_rows[:, q, :], x1[:, q, :]).then_inc(y_stored, 16)
            sp.wait_ge(y_stored, 16 * NQ)

        @block.gpsimd
        def _(pool):
            pool.wait_ge(l_condcol, 16)
            pool.indirect_dma_start(wsel[:, :], None, cond_w,
                                    bass.IndirectOffsetOnAxis(ap=cond_col[:, 0:1], axis=0),
                                    bounds_check=S - 1, oob_is_err=False).then_inc(wsel_here, 16)
            nc.gpsimd.memset(wbd[:, :, :], 0.0).then_inc(wbd_zero, 1)
            nc.gpsimd.memset(maskR[:, :, :], 0.0).then_inc(mask_zero, 1)
            nc.gpsimd.memset(qbd[:, :, :, :, :], 0.0).then_inc(qbd_zero, 1)
            nc.gpsimd.memset(PT2[:, :, :, :, :], 0.0).then_inc(pt2_zero, 1)
            pool.wait_ge(idx_cache_done, 1)
            for b in range(B):
                pool.indirect_dma_start(KV1[:, b, :], None, kv_rows,
                                        bass.IndirectOffsetOnAxis(ap=idx_cache[:, b:b + 1], axis=0),
                                        bounds_check=NPHYS * BLOCK - 1, oob_is_err=False
                                        ).then_inc(cache_here[b // QB], 16)
            pool.wait_ge(idx_new_done, 5)
            for g in range(NQ // GROUP):
                pool.wait_ge(rows_stored[g], 16)
            for q in range(NQ):
                pool.indirect_dma_start(KV2[:, q, :], None, new_rows,
                                        bass.IndirectOffsetOnAxis(ap=idx_tail[:, q:q + 1], axis=0),
                                        bounds_check=ROWS - 1, oob_is_err=False).then_inc(keys_here[q], 16)
                pool.wait_ge(cache_here[q], 16 * QB)
                for b in range(QB * q, QB * (q + 1)):
                    pool.indirect_dma_start(KV1[:, b, :], None, new_rows,
                                            bass.IndirectOffsetOnAxis(ap=idx_new[:, b:b + 1], axis=0),
                                            bounds_check=ROWS - 1, oob_is_err=False).then_inc(keys_here[q], 16)

        @block.scalar
        def _(act):
            act.dma_start(tab[:, :], four_times(tables)).then_inc(l_tab, 16)
            act.dma_start(cst[:, :], consts).then_inc(l_cst, 16)
            act.dma_start(kv_row[:, :], every_partition(kv_len, B)).then_inc(l_kvrow, 16)
            place_weights(act, 1)
            act.dma_start(nscale[:, 0, :], every_partition(q_scale, HD)).then_inc(l_scale, 16)
            act.dma_start(nscale[:, 1, :], every_partition(k_scale, HD)).then_inc(l_scale, 16)

            def copy_x1T(j):
                act.wait_ge(x1T_ps, j + 1)
                if j >= 2:
                    act.wait_ge(qkv_ps, j - 1)
                nc.scalar.copy(x1T[:, j % 2, :, :], ps_x1T[j % 2][:, 0:2 * P].rearrange("p (k m) -> p k m", k=2)
                               ).then_inc(x1T_done, 1)

            def split_qkv(j):
                act.wait_ge(qkv_ps, j + 1)
                nc.scalar.copy(raw[:, j, :], ps_qkv[j % 2][:, 0:NHK * HD]).then_inc(raw_done, 1)
                if j >= 4:
                    act.wait_ge(ss_done, j - 3)
                nc.scalar.activation(sq[:, j % 4, :, :],
                                     ps_qkv[j % 2][:, 0:NHK * HD].rearrange("p (h d) -> p h d", d=HD),
                                     ACT.Square).then_inc(sq_done, 1)
                nc.scalar.copy(newkv[:, j, G * HD:], ps_qkv[j % 2][:, NHK * HD:]).then_inc(newv_done, 1)

            def root(g):
                act.wait_ge(ms_done, g + 1)
                tiles = slice(GROUP * g, GROUP * (g + 1))
                nc.scalar.activation(rms[:, tiles, :], ms[:, tiles, :], ACT.Sqrt).then_inc(rms_done, 1)

            copy_x1T(0)
            for j in range(NQ):
                if j + 1 < NQ:
                    copy_x1T(j + 1)
                split_qkv(j)
                if j == 0:
                    act.wait_ge(entry_ps, 1)
                    n = OFFS * EN * QUAD
                    nc.scalar.copy(order_b[:, :, :], ps_entry[:, 0:n].rearrange("p (o e) -> p o e", o=OFFS)
                                   ).then_inc(entry_done, 1)
                    nc.scalar.copy(entry_b[:, :], ps_entry[:, n:n + EN * QUAD]).then_inc(entry_done, 1)
                if j == 2:
                    act.wait_ge(trig_arg, 1)
                    nc.scalar.activation(trig[:, :, :, :], ang[:, :, :, :], ACT.Sin).then_inc(trig_done, 1)
                if j == 5:
                    root(0)
            root(1)

            def place_q(q):
                act.wait_ge(kt_ps, q + 1)
                if q == 0:
                    act.wait_ge(qbd_zero, 1)
                if q >= 2:
                    act.wait_ge(score_ps, QB * (q - 1))
                for g in range(G):
                    rows = slice(QUAD * g, QUAD * (g + 1))
                    nc.scalar.copy(
                        qbd[rows, q % 2, :, g, :].rearrange("p b (h t) -> p b h t", h=H2),
                        ps_Q[rows, :].rearrange("p (h b t) -> p b h t", h=H2, b=QB)).then_inc(qbd_done, 1)

            def place_k(q):
                act.wait_ge(kt_ps, q + 1)
                if q >= 2:
                    act.wait_ge(score_ps, QB * (q - 1))
                nc.scalar.copy(KT[:, q % 2, :, 0:WINDOW], ps_KT[:, :].rearrange("p (b i) -> p b i", b=QB)
                               ).then_inc(kt_done, 1)
                nc.scalar.copy(KT[:, q % 2, :, WINDOW:], ps_KT2.rearrange("p (b i) -> p b i", b=QB)
                               ).then_inc(kt_done, 1)

            def exps(n):
                q, i = divmod(n, QB)
                act.wait_ge(max_done, n + 1)
                if q >= 2 and i == 0:
                    act.wait_ge(pt_ps, 2 * (q - 1))
                    act.wait_ge(tail_done, q - 1)
                for half in range(2):
                    nc.scalar.activation(Pm[:, q % 2, half, i, :],
                                         ps_S[n % 3][:, half, :], ACT.Exp,
                                         bias=nmax[:, n, half:half + 1],
                                         accum_out=psum_e[:, n, half:half + 1]).then_inc(exp_done, 1)

            def copy_pt(q, pair):
                act.wait_ge(pt_ps, 2 * q + pair + 1)
                if q >= 2:
                    act.wait_ge(ot_ps, q - 1)
                nc.scalar.copy(PT1[:, q % 2, 2 * pair:2 * pair + 2, :],
                               ps_PT[pair][:, :].rearrange("p (b n) -> p b n", b=2)).then_inc(pt_done, 1)

            def place_tails(q):
                act.wait_ge(pt2_ps, q + 1)
                if q == 0:
                    act.wait_ge(pt2_zero, 1)
                if q >= 2:
                    act.wait_ge(ot_ps, q - 1)
                for i in range(QB // 2):
                    rows = slice(QUAD * i, QUAD * (i + 1))
                    nc.scalar.copy(PT2[rows, q % 2, :, i, :],
                                   ps_PT2[rows, :].rearrange("p (g m) -> p g m", g=G)).then_inc(pt2_done, 1)

            def copy_ot(q):
                act.wait_ge(ot_ps, q + 1)
                if q >= 2:
                    act.wait_ge(y_ps, q - 1)
                nc.scalar.copy(oT[:, q % 2, :, :].rearrange("p h (b t) -> p b h t", b=QB),
                               ps_oT.rearrange("p (b h t) -> p b h t", b=QB, h=H2)).then_inc(ot_done, 1)

            place_q(0)
            place_k(0)
            for q in range(NQ):
                if q >= 1:
                    copy_pt(q - 1, 0)
                    place_tails(q - 1)
                for i in range(QB):
                    exps(QB * q + i)
                if q >= 1:
                    copy_ot(q - 1)
                if q + 1 < NQ:
                    place_q(q + 1)
                    place_k(q + 1)
            copy_pt(NQ - 1, 0)
            place_tails(NQ - 1)
            copy_ot(NQ - 1)

        @block.vector
        def _(dve):
            steps = [0]

            def link(ins):
                steps[0] += 1
                ins.then_inc(dve_own, 1)
                dve.wait_ge(dve_own, steps[0])

            dve.wait_ge(l_kv, 16 * 2)
            link(nc.vector.tensor_copy(kvi[:, 0:1], kv_col[:, :]))
            link(nc.vector.tensor_scalar(kvi[:, 1:2], kv_col[:, :], 1.0, None, ALU.add))
            dve.wait_ge(l_tab, 16)
            dve.wait_ge(l_cst, 16)
            nc.vector.tensor_scalar(kvs[:, :], kvi[:, :], 4, None, ALU.arith_shift_right).then_inc(dve_own, 1)
            nc.vector.tensor_scalar(kva[:, :], kvi[:, :], BLOCK - 1, None, ALU.bitwise_and).then_inc(dve_own, 1)
            steps[0] += 2
            link(nc.vector.tensor_copy(tabf[:, :], tab[:, :]))
            nc.vector.tensor_copy(kvf[:, 0:2], kvs[:, :]).then_inc(dve_own, 1)
            nc.vector.tensor_copy(kvf[:, 2:4], kva[:, :]).then_inc(dve_own, 1)
            nc.vector.tensor_tensor(bitf_i[:, :], kva[:, 1:2].to_broadcast([P, 4]), bits[:, :],
                                    ALU.bitwise_and).then_inc(dve_own, 1)
            steps[0] += 3
            dve.wait_ge(dve_own, steps[0])
            nc.vector.tensor_scalar(bitf[:, :], bitf_i[:, :], 0.0, None, ALU.is_gt).then_inc(dve_own, 1)
            steps[0] += 1
            link(nc.vector.tensor_scalar(slot_at[:, :], cst[:, where["slot_off"]], kvf[:, 1:2], None, ALU.add))
            for s in range(SLOTS):
                nc.vector.scalar_tensor_tensor(hit[:, s, :], cst[:, where["slots"]], slot_at[:, s:s + 1],
                                               tabf[:, :], ALU.is_equal, ALU.mult,
                                               accum_out=blk[:, s:s + 1]).then_inc(dve_own, 1)
                steps[0] += 1
            dve.wait_ge(dve_own, steps[0])

            def align(rows, done, between=None):
                n = SLOTS * BLOCK
                for k, by in enumerate((8, 4, 2, 1)):
                    n -= by
                    link(nc.vector.tensor_tensor(dshift[:, 0:n], rows[:, by:by + n], rows[:, 0:n], ALU.subtract))
                    ins = nc.vector.scalar_tensor_tensor(rows[:, 0:n], dshift[:, 0:n], bitf[0:B, k:k + 1],
                                                         rows[:, 0:n], ALU.mult, ALU.add)
                    if k < 3:
                        link(ins)
                        if k == 1 and between is not None:
                            between()
                    else:
                        ins.then_inc(done, 1)

            def place_diagonal():
                dve.wait_ge(wcd_here, 16 * NQ)
                dve.wait_ge(wbd_zero, 1)
                for c in range(QB):
                    rows = slice(QUAD * c, QUAD * (c + 1))
                    nc.vector.tensor_copy(wbd[rows, :, QUAD * c:QUAD * (c + 1)], wcd[rows, :, :]).then_inc(wbd_done, 1)

            def x1_rows(k):
                dve.wait_ge(x1_ps, k + 1)
                nc.vector.tensor_tensor(x1[:, 2 * k:2 * k + 2, :], ps_x1[k % 2][:, :].rearrange("p (j f) -> p j f", j=2),
                                        x_sb[:, 2 * k:2 * k + 2, :], ALU.add).then_inc(x1_done, 1)

            link(nc.vector.scalar_tensor_tensor(
                crow[:, :].rearrange("b (s o) -> b s o", o=BLOCK),
                blk[0:B, :].rearrange("b (s a) -> b s a", a=1).to_broadcast([B, SLOTS, BLOCK]), float(BLOCK),
                cst[0:B, where["key_off"]].rearrange("b (s o) -> b s o", o=BLOCK), ALU.mult, ALU.add))
            align(crow, crow_done, between=place_diagonal)
            dve.wait_ge(l_x, 16)
            x1_rows(0)

            dve.wait_ge(idx_ps, 1)
            nc.vector.tensor_copy(idx_cache[:, :], ps_idx[:, 0:B]).then_inc(idx_cache_done, 1)

            x1_rows(1)
            x1_rows(2)
            x1_rows(3)

            link(nc.vector.tensor_tensor(wrap[:, :], kvf[:, 1:2], kvf[:, 0:1], ALU.subtract))
            nc.vector.tensor_scalar(tnew[:, :], cst[:, where["new_off"]], kvf[:, 2:3], None,
                                    ALU.subtract).then_inc(dve_own, 1)
            steps[0] += 1
            link(nc.vector.tensor_tensor(dblk[:, :], blk[:, 7:7 + EN], blk[:, 8:8 + EN], ALU.subtract))
            nc.vector.scalar_tensor_tensor(WM[:, OFFS * EN:], dblk[:, :], wrap[:, 0:1], blk[:, 8:8 + EN],
                                           ALU.mult, ALU.add).then_inc(dve_own, 1)
            steps[0] += 1
            link(nc.vector.tensor_scalar(tge[:, :], tnew[:, :], 0.0, None, ALU.is_ge))
            link(nc.vector.scalar_tensor_tensor(tin[:, :], tnew[:, :], float(C - 1), tge[:, :],
                                                ALU.is_le, ALU.mult))
            link(nc.vector.scalar_tensor_tensor(WM[:, 0:OFFS * EN], tnew[:, :], cst[:, where["order"]], tin[:, :],
                                                ALU.add, ALU.mult))
            nw = OFFS * EN + EN
            nc.vector.tensor_tensor(
                spread[:, :, :], WM[:, :].rearrange("p (w a) -> p w a", a=1).to_broadcast([P, nw, QUAD]),
                eye32.rearrange("p (a n) -> p a n", a=1).to_broadcast([P, nw, QUAD]), ALU.mult
            ).then_inc(spread_done, 1)

            dve.wait_ge(l_kvrow, 16)
            for c in range(QB):
                rows = slice(QUAD * c, QUAD * (c + 1))
                ins = nc.vector.tensor_scalar(posf[rows, :], kv_row[rows, c:B:QB],
                                              cst[rows, where["row_in_tile"]], None, ALU.add)
                ins.then_inc(dve_own, 1)
                steps[0] += 1
            dve.wait_ge(dve_own, steps[0])
            nh = HD // 2
            for part in range(2):
                nc.vector.tensor_tensor(
                    ang[:, part, :, :], posf[:, :].rearrange("p (j a) -> p j a", a=1).to_broadcast([P, NQ, nh]),
                    cst[:, where["inv_freq"]].rearrange("p (a f) -> p a f", a=1).to_broadcast([P, NQ, nh]),
                    ALU.mult).then_inc(dve_own, 1)
                steps[0] += 1
            dve.wait_ge(dve_own, steps[0])
            link(nc.vector.tensor_scalar(turns[:, 0, :, :], ang[:, 0, :, :], INV_2PI, None, ALU.mult))
            link(nc.vector.tensor_scalar(turns[:, 1, :, :], turns[:, 0, :, :], 0.25, MAGIC, ALU.add, ALU.add))
            link(nc.vector.tensor_scalar(turns[:, 0, :, :], turns[:, 0, :, :], MAGIC, None, ALU.add))
            link(nc.vector.tensor_scalar(turns[:, :, :, :], turns[:, :, :, :], MAGIC, None, ALU.subtract))
            for part in (C1, C2, C3):
                link(nc.vector.scalar_tensor_tensor(ang[:, :, :, :], turns[:, :, :, :], -part, ang[:, :, :, :],
                                                    ALU.mult, ALU.add))
            link(nc.vector.tensor_scalar(ang[:, 1, :, :], ang[:, 1, :, :], PI / 2, None, ALU.add))
            nc.vector.tensor_scalar(ang[:, :, :, :], ang[:, :, :, :], PI, -PI, ALU.min, ALU.max).then_inc(trig_arg, 1)


            def sum_squares(j):
                dve.wait_ge(sq_done, j + 1)
                nc.vector.tensor_reduce(ss[:, j, :], sq[:, j % 4, :, :], X, ALU.add).then_inc(ss_done, 1)

            def mean_squares(g):
                tiles = slice(GROUP * g, GROUP * (g + 1))
                dve.wait_ge(ss_done, GROUP * (g + 1))
                link(nc.vector.tensor_scalar(ms[:, tiles, :], ss[:, tiles, :], 1.0 / HD, EPS, ALU.mult, ALU.add))
                nc.vector.reciprocal(ms[:, tiles, :], ms[:, tiles, :]).then_inc(ms_done, 1)

            def rotate_k(g):
                tiles = slice(GROUP * g, GROUP * (g + 1))
                dve.wait_ge(raw_done, GROUP * (g + 1))
                src = raw[:, tiles, H * HD:].rearrange("p j (h d) -> p j h d", d=HD)

                def table(t, lo, hi):
                    return t[:, 1, tiles, lo:hi].rearrange("p j (a d) -> p j a d", a=1).to_broadcast(
                        [P, GROUP, G, hi - lo])

                nc.vector.tensor_tensor(rk1[:, :, :, :], src, table(cosw, 0, HD), ALU.mult).then_inc(dve_own, 1)
                nc.vector.tensor_tensor(rk2[:, :, :, 0:nh], src[:, :, :, nh:], table(sinw, 0, nh),
                                        ALU.mult).then_inc(dve_own, 1)
                steps[0] += 2
                link(nc.vector.tensor_tensor(rk2[:, :, :, nh:], src[:, :, :, 0:nh], table(sinw, nh, HD), ALU.mult))
                link(nc.vector.tensor_tensor(rkd[:, tiles, :, :], rk1[:, :, :, :], rk2[:, :, :, :], ALU.add))

            def finish_k(g):
                tiles = slice(GROUP * g, GROUP * (g + 1))
                dve.wait_ge(rms_done, g + 1)
                nc.vector.tensor_tensor(
                    newkv[:, tiles, 0:G * HD].rearrange("p j (h d) -> p j h d", d=HD), rkd[:, tiles, :, :],
                    rms[:, tiles, H:].rearrange("p j (h a) -> p j h a", a=1).to_broadcast([P, GROUP, G, HD]),
                    ALU.mult).then_inc(newk_done, 1)

            dve.wait_ge(entry_done, 2)
            ne = EN * QUAD
            link(nc.vector.tensor_tensor(
                same[:, :, :], blk[:, :].rearrange("p (s a) -> p s a", a=1).to_broadcast([P, SLOTS, ne]),
                entry_b[:, :].rearrange("p (a e) -> p a e", a=1).to_broadcast([P, SLOTS, ne]), ALU.is_equal))
            sum_squares(0)
            link(nc.vector.tensor_tensor(
                cand[:, :, :, :],
                same[:, :, :].rearrange("p s (a e) -> p s a e", a=1).to_broadcast([P, SLOTS, OFFS, ne]),
                order_b[:, :, :].rearrange("p (a o) e -> p a o e", a=1).to_broadcast([P, SLOTS, OFFS, ne]),
                ALU.mult))
            sum_squares(1)
            sum_squares(2)
            n = ne
            while n % 2 == 0 and n > 6:
                n //= 2
                link(nc.vector.tensor_tensor(cand[:, :, :, 0:n], cand[:, :, :, 0:n], cand[:, :, :, n:2 * n], ALU.max))
            link(nc.vector.tensor_reduce(win[:, :, :], cand[:, :, :, 0:n], X, ALU.max))
            dve.wait_ge(l_scale, 32)
            link(nc.vector.tensor_scalar(w1p[:, :, :], nscale[:, :, :], 1.0, None, ALU.add))
            link(nc.vector.tensor_scalar(w1p[:, 0, :], w1p[:, 0, :], SCALE, None, ALU.mult))
            link(nc.vector.tensor_scalar(wneg[:, :, :], w1p[:, :, nh:], -1.0, None, ALU.mult))
            dve.wait_ge(trig_done, 1)

            def per_tile(w):
                return w.rearrange("p (a f) -> p a f", a=1).to_broadcast([P, NQ, nh])

            for part in range(2):
                for lo in (0, nh):
                    nc.vector.tensor_tensor(cosw[:, part, :, lo:lo + nh], trig[:, 1, :, :],
                                            per_tile(w1p[:, part, lo:lo + nh]), ALU.mult).then_inc(dve_own, 1)
                nc.vector.tensor_tensor(sinw[:, part, :, 0:nh], trig[:, 0, :, :],
                                        per_tile(wneg[:, part, :]), ALU.mult).then_inc(dve_own, 1)
                nc.vector.tensor_tensor(sinw[:, part, :, nh:], trig[:, 0, :, :],
                                        per_tile(w1p[:, part, 0:nh]), ALU.mult).then_inc(dve_own, 1)
                steps[0] += 4
            dve.wait_ge(dve_own, steps[0])

            sum_squares(3)
            mean_squares(0)
            rotate_k(0)
            sum_squares(4)
            for c in range(4):
                nc.vector.tensor_copy(
                    wkey[:, :].rearrange("b (s c o) -> b s c o", c=4, o=OFFS)[:, :, c, :],
                    win[QUAD * c:QUAD * (c + 1), :, :]).then_inc(dve_own, 1)
                steps[0] += 1
            dve.wait_ge(dve_own, steps[0])
            link(nc.vector.tensor_scalar(wnone[:, :], wkey[:, :], 0.0, float(NO_WINNER), ALU.is_equal, ALU.mult))
            link(nc.vector.scalar_tensor_tensor(wkey[:, :], wkey[:, :], -1.0, wnone[:, :], ALU.add, ALU.add))
            dve.wait_ge(crow_done, 1)
            align(wkey, wkey_done)
            sum_squares(5)
            finish_k(0)
            link(nc.vector.tensor_scalar(lack[:, :], kv_col[0:B, :], -1.0, float(WINDOW - 1), ALU.mult, ALU.add))
            nc.vector.tensor_scalar(dmask[:, :], cst[0:B, where["slots"]][:, 0:KEYS], lack[:, 0:1], NEG,
                                    ALU.is_lt, ALU.mult).then_inc(dmask_done, 1)
            sum_squares(6)
            sum_squares(7)
            mean_squares(1)
            rotate_k(1)
            finish_k(1)
            dve.wait_ge(idx_ps, 2)
            nc.vector.tensor_copy(idx_new[:, :], ps_idx[:, B:2 * B]).then_inc(idx_new_done, 1)
            for c in range(QB):
                nc.vector.tensor_scalar(idx_tail[QUAD * c:QUAD * (c + 1), :], ps_idx[0:QUAD, 2 * B + c:3 * B:QB],
                                        float(ROWS - 1), None, ALU.min).then_inc(idx_new_done, 1)

            def finish_q(tiles):
                n = tiles.stop - tiles.start
                src = raw[:, tiles, 0:H * HD].rearrange("p j (h d) -> p j h d", d=HD)

                def table(t, lo, hi):
                    return t[:, 0, tiles, lo:hi].rearrange("p j (a d) -> p j a d", a=1).to_broadcast([P, n, H, hi - lo])

                nc.vector.tensor_tensor(rq1[:, 0:n, :, :], src, table(cosw, 0, HD), ALU.mult).then_inc(dve_own, 1)
                nc.vector.tensor_tensor(rq2[:, 0:n, :, 0:nh], src[:, :, :, nh:], table(sinw, 0, nh),
                                        ALU.mult).then_inc(dve_own, 1)
                steps[0] += 2
                link(nc.vector.tensor_tensor(rq2[:, 0:n, :, nh:], src[:, :, :, 0:nh], table(sinw, nh, HD), ALU.mult))
                link(nc.vector.tensor_tensor(rq1[:, 0:n, :, :], rq1[:, 0:n, :, :], rq2[:, 0:n, :, :], ALU.add))
                nc.vector.tensor_tensor(
                    qrows[:, tiles, :].rearrange("p j (h d) -> p j h d", d=HD), rq1[:, 0:n, :, :],
                    rms[:, tiles, 0:H].rearrange("p j (h a) -> p j h a", a=1).to_broadcast([P, n, H, HD]),
                    ALU.mult).then_inc(qrow_done, 1)
                dve.wait_ge(qrow_done, Q_GROUPS.index(tiles) + 1)

            def row_max(n):
                dve.wait_ge(score_ps, n + 1)
                nc.vector.tensor_reduce(nmax[:, n, :],
                                        ps_S[n % 3], X, ALU.max, negate=True).then_inc(max_done, 1)

            def normalise(n):
                q, i = divmod(n, QB)
                if i % 2 == 0:
                    dve.wait_ge(exp_done, 2 * (n + 2))
                    link(nc.vector.reciprocal(rsum[:, n:n + 2, :], psum_e[:, n:n + 2, :]))
                for half in range(2):
                    nc.vector.tensor_scalar(Pm[:, q % 2, half, i, 0:WINDOW], Pm[:, q % 2, half, i, 0:WINDOW],
                                            rsum[:, n, half:half + 1], None, ALU.mult).then_inc(norm_done, 1)

            def normalise_tails(q):
                if q >= 2:
                    dve.wait_ge(pt2_ps, q - 1)
                nc.vector.tensor_tensor(
                    Ptail[:, q % 2, :, :, :], Pm[:, q % 2, :, :, WINDOW:],
                    rsum[:, QB * q:QB * (q + 1), :].rearrange("p (a b) h -> p h b a", a=1).to_broadcast(
                        [P, 2, QB, KEYS - WINDOW]), ALU.mult).then_inc(tail_done, 1)

            def copy_pt(q, pair):
                dve.wait_ge(pt_ps, 2 * q + pair + 1)
                if q >= 2:
                    dve.wait_ge(ot_ps, q - 1)
                nc.vector.tensor_copy(PT1[:, q % 2, 2 * pair:2 * pair + 2, :],
                                      ps_PT[pair][:, :].rearrange("p (b n) -> p b n", b=2)).then_inc(ptb_done, 1)

            def place_tails(q):
                dve.wait_ge(pt2_ps, q + 1)
                if q == 0:
                    dve.wait_ge(pt2_zero, 1)
                if q >= 2:
                    dve.wait_ge(ot_ps, q - 1)
                for i in range(QB // 2, QB):
                    rows = slice(QUAD * i, QUAD * (i + 1))
                    nc.vector.tensor_copy(PT2[rows, q % 2, :, i, :],
                                          ps_PT2[rows, :].rearrange("p (g m) -> p g m", g=G)).then_inc(ptb2_done, 1)

            def finish_y(q):
                dve.wait_ge(y_ps, q + 1)
                nc.vector.tensor_tensor(x1[:, q, :], ps_y, x1[:, q, :], ALU.add).then_inc(y_done, 1)

            for tiles in Q_GROUPS:
                finish_q(tiles)
            for q in range(NQ):
                if q >= 1:
                    copy_pt(q - 1, 1)
                    place_tails(q - 1)
                row_max(QB * q)
                row_max(QB * q + 1)
                if q >= 2:
                    finish_y(q - 2)
                row_max(QB * q + 2)
                row_max(QB * q + 3)
                for i in range(QB):
                    normalise(QB * q + i)
                normalise_tails(q)
            copy_pt(NQ - 1, 1)
            place_tails(NQ - 1)
            finish_y(NQ - 2)
            finish_y(NQ - 1)

        @block.tensor
        def _(pe):
            def x1_rows(k):
                if k >= 2:
                    pe.wait_ge(x1_done, k - 1)
                for j in (2 * k, 2 * k + 1):
                    last = nc.tensor.matmul(ps_x1[k % 2][:, T * (j % 2):T * (j % 2 + 1)], wbd[:, j, :], x_sb[:, j, :],
                                            start=True, stop=True)
                last.then_inc(x1_ps, 1)

            def x1_columns(j):
                pe.wait_ge(x1_done, j // 2 + 1)
                if j >= 2:
                    pe.wait_ge(x1T_done, j - 1)
                for k in range(2):
                    last = nc.tensor.transpose(ps_x1T[j % 2][:, P * k:P * (k + 1)],
                                               x1[:, j, P * k:P * (k + 1)], ident)
                last.then_inc(x1T_ps, 1)

            def project(j):
                pe.wait_ge(x1T_done, j + 1)
                if j >= 2:
                    pe.wait_ge(newv_done, j - 1)
                for k in range(2):
                    last = nc.tensor.matmul(ps_qkv[j % 2][:, :], x1T[:, j % 2, k, :], wqkv_sb[:, k, :],
                                            start=(k == 0), stop=(k == 1))
                last.then_inc(qkv_ps, 1)

            pe.wait_ge(wbd_done, QB)
            pe.wait_ge(l_x, 16)
            x1_rows(0)
            x1_rows(1)
            pe.wait_ge(l_cst, 16)
            pe.wait_ge(crow_done, 1)
            nc.tensor.transpose(ps_idx[:, 0:B], crow[:, 0:WINDOW], ident[0:B, 0:B]).then_inc(idx_ps, 1)
            x1_columns(0)
            x1_rows(2)
            pe.wait_ge(l_wqkv, 16)
            for j in range(NQ):
                if j + 1 < NQ:
                    x1_columns(j + 1)
                if j == 0:
                    x1_rows(3)
                project(j)
                if j == 0:
                    pe.wait_ge(spread_done, 1)
                    nc.tensor.matmul(ps_entry[:, 0:(OFFS * EN + EN) * QUAD], cst[:, where["blockones"]],
                                     spread[:, :, :].rearrange("p w n -> p (w n)"), start=True, stop=True
                                     ).then_inc(entry_ps, 1)
            pe.wait_ge(wkey_done, 1)
            pe.wait_ge(idx_cache_done, 1)
            nc.tensor.transpose(ps_idx[:, B:2 * B], wkey[:, 0:WINDOW], ident[0:B, 0:B])
            nc.tensor.transpose(ps_idx[0:C, 2 * B:3 * B], wkey[:, WINDOW:KEYS], ident[0:B, 0:B]).then_inc(idx_ps, 1)

            def q_columns(q):
                pe.wait_ge(qrow_done, 1 + next(k for k, tiles in enumerate(Q_GROUPS) if q < tiles.stop))
                if q >= 1:
                    pe.wait_ge(qbd_done, G * q)
                    pe.wait_ge(kt_done, 2 * q)
                for h in range(H2):
                    last = nc.tensor.transpose(ps_Q[:, P * h:P * (h + 1)], qrows[:, q, P * h:P * (h + 1)], ident)
                last.then_inc(q_ps, 1)

            def k_columns(q):
                pe.wait_ge(keys_here[q], 16 * (QB + 1))
                if q >= 1:
                    pe.wait_ge(kt_done, 2 * q)
                for i in range(QB):
                    nc.tensor.transpose(ps_KT[:, P * i:P * (i + 1)], KV1[:, QB * q + i, 0:G * HD], ident)
                nc.tensor.transpose(ps_KT2, KV2[:, q, 0:G * HD], ident).then_inc(kt_ps, 1)

            def scores(n):
                q, i = divmod(n, QB)
                if i == 0:
                    pe.wait_ge(qbd_done, G * (q + 1))
                    pe.wait_ge(kt_done, 2 * (q + 1))
                if n == 0:
                    pe.wait_ge(l_mask, 16 * 2)
                    pe.wait_ge(dmask_here, 16)
                if n >= 3:
                    pe.wait_ge(exp_done, 2 * (n - 2))
                nc.tensor.matmul(ps_S[n % 3], maskL[:, :],
                                 maskR[:, n, :].rearrange("p (a i) -> p a i", a=1).to_broadcast([P, 2, KEYS]),
                                 start=True, stop=False, skip_group_check=True)
                for half in range(2):
                    last = nc.tensor.matmul(ps_S[n % 3][:, half, :],
                                            qbd[:, q % 2, i, 2 * half:2 * half + 2, :].rearrange("p g m -> p (g m)"),
                                            KT[:, q % 2, i, :], start=False, stop=True, skip_group_check=True)
                last.then_inc(score_ps, 1)

            def p_columns(q, pair):
                pe.wait_ge(norm_done, 2 * (QB * q + 2 * pair + 2))
                if q >= 1:
                    pe.wait_ge(ptb_done if pair else pt_done, q)
                for k in range(2):
                    for half in range(2):
                        c = (2 * k + half) * P
                        last = nc.tensor.transpose(ps_PT[pair][:, c:c + P],
                                                   Pm[:, q % 2, half, 2 * pair + k, 0:WINDOW], ident)
                last.then_inc(pt_ps, 1)

            def p_tail_columns(q):
                pe.wait_ge(tail_done, q + 1)
                if q >= 1:
                    pe.wait_ge(ot_done, q)
                for half in range(2):
                    last = nc.tensor.transpose(ps_PT2[:, P * half:P * (half + 1)],
                                               Ptail[:, q % 2, half, :, :].rearrange("p b i -> p (b i)"), ident)
                last.then_inc(pt2_ps, 1)

            def values(q, pair):
                if pair == 0:
                    pe.wait_ge(pt_done, q + 1)
                    pe.wait_ge(ptb_done, q + 1)
                    pe.wait_ge(pt2_done, QB // 2 * (q + 1))
                    pe.wait_ge(ptb2_done, QB // 2 * (q + 1))
                    if q >= 1:
                        pe.wait_ge(y_done, q)
                if pair == 0:
                    for g in range(G):
                        nc.tensor.matmul(ps_oT[QUAD * g:QUAD * (g + 1), :],
                                         KV2[:, q, HD * (G + g):HD * (G + g + 1)],
                                         PT2[:, q % 2, g, :, :].rearrange("p b m -> p (b m)"),
                                         start=True, stop=False, skip_group_check=True)
                for i in (2 * pair, 2 * pair + 1):
                    for g in range(G):
                        last = nc.tensor.matmul(ps_oT[QUAD * g:QUAD * (g + 1), 64 * i:64 * (i + 1)],
                                                KV1[:, QB * q + i, HD * (G + g):HD * (G + g + 1)],
                                                PT1[:, q % 2, i, 64 * g:64 * (g + 1)],
                                                start=False, stop=True, skip_group_check=True)
                if pair == 1:
                    last.then_inc(ot_ps, 1)

            def output(q):
                if q == 0:
                    pe.wait_ge(l_wo, 16)
                pe.wait_ge(ot_done, q + 1)
                if q + 1 < NQ:
                    pe.wait_ge(pt2_done, QB // 2 * (q + 2))
                    pe.wait_ge(ptb2_done, QB // 2 * (q + 2))
                for h in range(H2):
                    last = nc.tensor.matmul(ps_y, oT[:, q % 2, h, :], wo_sb[:, h, :], start=(h == 0), stop=(h == 1))
                last.then_inc(y_ps, 1)

            pe.wait_ge(newv_done, NQ)
            pe.wait_ge(idx_new_done, 5)
            pe.wait_ge(entry_done, 2)
            q_columns(0)
            k_columns(0)
            for q in range(NQ):
                scores(QB * q)
                scores(QB * q + 1)
                if q >= 2:
                    output(q - 2)
                scores(QB * q + 2)
                scores(QB * q + 3)
                if q + 1 < NQ:
                    q_columns(q + 1)
                    k_columns(q + 1)
                if q >= 1:
                    values(q - 1, 0)
                    values(q - 1, 1)
                p_columns(q, 0)
                p_columns(q, 1)
                p_tail_columns(q)
            output(NQ - 2)
            values(NQ - 1, 0)
            values(NQ - 1, 1)
            output(NQ - 1)


def kernel(x, itok_B_1_198, itok_Bx257_0_4111, itok_B_37_3939, L0_cond_weights, L1_cond_Wq, L1_cond_Wk,
           L1_cond_Wv, L1_cond_Wo, L1_cond_q_norm_scale, L1_cond_k_norm_scale, L1_cond_k_blocks,
           L1_cond_v_blocks):
    import concourse.bacc as bacc
    import ml_dtypes
    from concourse.bass_utils import run_bass_kernel_spmd as run

    def q_order(w):
        return np.asarray(w).reshape(G, H2, HD, -1).transpose(1, 0, 2, 3).reshape(H * HD, -1)

    wo_T = np.asarray(L1_cond_Wo).T
    mask_left, mask_band = mask_constants()
    arrays = {
        "x": np.asarray(x).reshape(ROWS, T),
        "cond": np.asarray(itok_B_1_198),
        "kv_len": np.asarray(itok_B_37_3939),
        "tables": np.asarray(itok_Bx257_0_4111),
        "cond_w": np.asarray(L0_cond_weights).reshape(S, C * C),
        "w_qkv": np.concatenate([q_order(L1_cond_Wq).T, np.asarray(L1_cond_Wk).T, np.asarray(L1_cond_Wv).T], axis=1),
        "w_o": q_order(wo_T),
        "q_scale": np.asarray(L1_cond_q_norm_scale),
        "k_scale": np.asarray(L1_cond_k_norm_scale),
        "kv_rows": np.concatenate([np.asarray(a).transpose(0, 2, 1, 3).reshape(NPHYS * BLOCK, G * HD)
                                   for a in (L1_cond_k_blocks, L1_cond_v_blocks)], axis=1),
        "consts": constants(),
        "mask_left": mask_left.astype(ml_dtypes.bfloat16),
        "mask_band": mask_band.astype(ml_dtypes.bfloat16),
        "bit_values": np.tile(np.array([[8, 4, 2, 1]], np.int32), (P, 1)),
    }
    nc = bacc.Bacc("TRN2", target_bir_lowering=False, num_devices=1)
    arrays = {k: np.ascontiguousarray(a) for k, a in arrays.items()}
    aps = [nc.dram_tensor(k, a.shape, mybir.dt.from_np(a.dtype), kind="ExternalInput").ap()
           for k, a in arrays.items()]
    out = nc.dram_tensor("out", (ROWS, T), F32, kind="ExternalOutput").ap()
    new_rows = nc.dram_tensor("new_rows", (ROWS, 2 * G * HD), F32, kind="Internal").ap()
    dyn_mask = nc.dram_tensor("dyn_mask", (B, KEYS), BF16, kind="Internal").ap()
    build(nc, *aps, out, new_rows, dyn_mask)
    r = run(nc, [arrays], core_ids=[0])
    return r.results[0]["out"].reshape(B, C, T)
```
